# Optimizing a Trainium2 kernel written in Bass

```python
import numpy as np
import jax
import jax.numpy as jnp

def _softmax(x, axis=-1):
    return jax.nn.softmax(x, axis=axis)

def _gelu(x):
    return jax.nn.gelu(x, approximate=True)

def _silu(x):
    return jax.nn.silu(x)

def _sigmoid(x):
    return jax.nn.sigmoid(x)

def _layernorm(x, axis=-1, eps=1e-05):
    m = jnp.mean(x, axis=axis, keepdims=True)
    v = jnp.var(x, axis=axis, keepdims=True)
    return (x - m) / jnp.sqrt(v + eps)

def _scatter_add(tgt, idx, src, axis=0):
    return tgt.at[idx].add(src)

def _segment_sum(src, seg, n):
    return jax.ops.segment_sum(src, seg, n)
kernel_name = 'mk_dlrm_tower_d1_rec_r8_6b499e'

def setup_inputs(seed: int=0):
    np.random.seed(seed)
    _w = jnp.asarray

    def _rec_inputs():
        import jax
        import jax.numpy as jnp
        _tk = jax.random.key(seed)
        dense_ctx = jax.random.normal(jax.random.fold_in(_tk, 190), (512, 16), jnp.float32)
        ids = jnp.stack([jax.random.randint(jax.random.fold_in(_tk, 200 + f), (512,), 0, v, jnp.int32) for f, v in enumerate([1250, 125000, 1250, 1000, 125000, 1000, 12500, 12500, 125000, 125000, 12500, 125000, 1250, 12500, 1000, 125000, 12500, 1000, 1000, 1000, 12500, 125000, 1000, 125000, 125000, 125000, 12500, 125000, 1250, 1000, 1000, 1000, 125000, 12500, 12500, 1250, 12500, 125000, 1000, 12500, 125000, 12500, 12500, 12500, 12500, 1250, 1000, 1000, 1250, 1000, 1000, 1250, 1250, 1250, 1000, 1000, 1000, 1000, 1000, 1000, 1000, 1000, 1000, 1000])], axis=1)
        tbl_0 = 0.05 * jax.random.normal(jax.random.fold_in(_tk, 500 + 0), (1250, 16), jnp.float32)
        tbl_1 = 0.05 * jax.random.normal(jax.random.fold_in(_tk, 500 + 1), (125000, 16), jnp.float32)
        tbl_2 = 0.05 * jax.random.normal(jax.random.fold_in(_tk, 500 + 2), (1250, 16), jnp.float32)
        tbl_3 = 0.05 * jax.random.normal(jax.random.fold_in(_tk, 500 + 3), (1000, 16), jnp.float32)
        tbl_4 = 0.05 * jax.random.normal(jax.random.fold_in(_tk, 500 + 4), (125000, 16), jnp.float32)
        tbl_5 = 0.05 * jax.random.normal(jax.random.fold_in(_tk, 500 + 5), (1000, 16), jnp.float32)
        tbl_6 = 0.05 * jax.random.normal(jax.random.fold_in(_tk, 500 + 6), (12500, 16), jnp.float32)
        tbl_7 = 0.05 * jax.random.normal(jax.random.fold_in(_tk, 500 + 7), (12500, 16), jnp.float32)
        tbl_8 = 0.05 * jax.random.normal(jax.random.fold_in(_tk, 500 + 8), (125000, 16), jnp.float32)
        tbl_9 = 0.05 * jax.random.normal(jax.random.fold_in(_tk, 500 + 9), (125000, 16), jnp.float32)
        tbl_10 = 0.05 * jax.random.normal(jax.random.fold_in(_tk, 500 + 10), (12500, 16), jnp.float32)
        tbl_11 = 0.05 * jax.random.normal(jax.random.fold_in(_tk, 500 + 11), (125000, 16), jnp.float32)
        tbl_12 = 0.05 * jax.random.normal(jax.random.fold_in(_tk, 500 + 12), (1250, 16), jnp.float32)
        tbl_13 = 0.05 * jax.random.normal(jax.random.fold_in(_tk, 500 + 13), (12500, 16), jnp.float32)
        tbl_14 = 0.05 * jax.random.normal(jax.random.fold_in(_tk, 500 + 14), (1000, 16), jnp.float32)
        tbl_15 = 0.05 * jax.random.normal(jax.random.fold_in(_tk, 500 + 15), (125000, 16), jnp.float32)
        tbl_16 = 0.05 * jax.random.normal(jax.random.fold_in(_tk, 500 + 16), (12500, 16), jnp.float32)
        tbl_17 = 0.05 * jax.random.normal(jax.random.fold_in(_tk, 500 + 17), (1000, 16), jnp.float32)
        tbl_18 = 0.05 * jax.random.normal(jax.random.fold_in(_tk, 500 + 18), (1000, 16), jnp.float32)
        tbl_19 = 0.05 * jax.random.normal(jax.random.fold_in(_tk, 500 + 19), (1000, 16), jnp.float32)
        tbl_20 = 0.05 * jax.random.normal(jax.random.fold_in(_tk, 500 + 20), (12500, 16), jnp.float32)
        tbl_21 = 0.05 * jax.random.normal(jax.random.fold_in(_tk, 500 + 21), (125000, 16), jnp.float32)
        tbl_22 = 0.05 * jax.random.normal(jax.random.fold_in(_tk, 500 + 22), (1000, 16), jnp.float32)
        tbl_23 = 0.05 * jax.random.normal(jax.random.fold_in(_tk, 500 + 23), (125000, 16), jnp.float32)
        tbl_24 = 0.05 * jax.random.normal(jax.random.fold_in(_tk, 500 + 24), (125000, 16), jnp.float32)
        tbl_25 = 0.05 * jax.random.normal(jax.random.fold_in(_tk, 500 + 25), (125000, 16), jnp.float32)
        tbl_26 = 0.05 * jax.random.normal(jax.random.fold_in(_tk, 500 + 26), (12500, 16), jnp.float32)
        tbl_27 = 0.05 * jax.random.normal(jax.random.fold_in(_tk, 500 + 27), (125000, 16), jnp.float32)
        tbl_28 = 0.05 * jax.random.normal(jax.random.fold_in(_tk, 500 + 28), (1250, 16), jnp.float32)
        tbl_29 = 0.05 * jax.random.normal(jax.random.fold_in(_tk, 500 + 29), (1000, 16), jnp.float32)
        tbl_30 = 0.05 * jax.random.normal(jax.random.fold_in(_tk, 500 + 30), (1000, 16), jnp.float32)
        tbl_31 = 0.05 * jax.random.normal(jax.random.fold_in(_tk, 500 + 31), (1000, 16), jnp.float32)
        tbl_32 = 0.05 * jax.random.normal(jax.random.fold_in(_tk, 500 + 32), (125000, 16), jnp.float32)
        tbl_33 = 0.05 * jax.random.normal(jax.random.fold_in(_tk, 500 + 33), (12500, 16), jnp.float32)
        tbl_34 = 0.05 * jax.random.normal(jax.random.fold_in(_tk, 500 + 34), (12500, 16), jnp.float32)
        tbl_35 = 0.05 * jax.random.normal(jax.random.fold_in(_tk, 500 + 35), (1250, 16), jnp.float32)
        tbl_36 = 0.05 * jax.random.normal(jax.random.fold_in(_tk, 500 + 36), (12500, 16), jnp.float32)
        tbl_37 = 0.05 * jax.random.normal(jax.random.fold_in(_tk, 500 + 37), (125000, 16), jnp.float32)
        tbl_38 = 0.05 * jax.random.normal(jax.random.fold_in(_tk, 500 + 38), (1000, 16), jnp.float32)
        tbl_39 = 0.05 * jax.random.normal(jax.random.fold_in(_tk, 500 + 39), (12500, 16), jnp.float32)
        tbl_40 = 0.05 * jax.random.normal(jax.random.fold_in(_tk, 500 + 40), (125000, 16), jnp.float32)
        tbl_41 = 0.05 * jax.random.normal(jax.random.fold_in(_tk, 500 + 41), (12500, 16), jnp.float32)
        tbl_42 = 0.05 * jax.random.normal(jax.random.fold_in(_tk, 500 + 42), (12500, 16), jnp.float32)
        tbl_43 = 0.05 * jax.random.normal(jax.random.fold_in(_tk, 500 + 43), (12500, 16), jnp.float32)
        tbl_44 = 0.05 * jax.random.normal(jax.random.fold_in(_tk, 500 + 44), (12500, 16), jnp.float32)
        tbl_45 = 0.05 * jax.random.normal(jax.random.fold_in(_tk, 500 + 45), (1250, 16), jnp.float32)
        tbl_46 = 0.05 * jax.random.normal(jax.random.fold_in(_tk, 500 + 46), (1000, 16), jnp.float32)
        tbl_47 = 0.05 * jax.random.normal(jax.random.fold_in(_tk, 500 + 47), (1000, 16), jnp.float32)
        tbl_48 = 0.05 * jax.random.normal(jax.random.fold_in(_tk, 500 + 48), (1250, 16), jnp.float32)
        tbl_49 = 0.05 * jax.random.normal(jax.random.fold_in(_tk, 500 + 49), (1000, 16), jnp.float32)
        tbl_50 = 0.05 * jax.random.normal(jax.random.fold_in(_tk, 500 + 50), (1000, 16), jnp.float32)
        tbl_51 = 0.05 * jax.random.normal(jax.random.fold_in(_tk, 500 + 51), (1250, 16), jnp.float32)
        tbl_52 = 0.05 * jax.random.normal(jax.random.fold_in(_tk, 500 + 52), (1250, 16), jnp.float32)
        tbl_53 = 0.05 * jax.random.normal(jax.random.fold_in(_tk, 500 + 53), (1250, 16), jnp.float32)
        tbl_54 = 0.05 * jax.random.normal(jax.random.fold_in(_tk, 500 + 54), (1000, 16), jnp.float32)
        tbl_55 = 0.05 * jax.random.normal(jax.random.fold_in(_tk, 500 + 55), (1000, 16), jnp.float32)
        tbl_56 = 0.05 * jax.random.normal(jax.random.fold_in(_tk, 500 + 56), (1000, 16), jnp.float32)
        tbl_57 = 0.05 * jax.random.normal(jax.random.fold_in(_tk, 500 + 57), (1000, 16), jnp.float32)
        tbl_58 = 0.05 * jax.random.normal(jax.random.fold_in(_tk, 500 + 58), (1000, 16), jnp.float32)
        tbl_59 = 0.05 * jax.random.normal(jax.random.fold_in(_tk, 500 + 59), (1000, 16), jnp.float32)
        tbl_60 = 0.05 * jax.random.normal(jax.random.fold_in(_tk, 500 + 60), (1000, 16), jnp.float32)
        tbl_61 = 0.05 * jax.random.normal(jax.random.fold_in(_tk, 500 + 61), (1000, 16), jnp.float32)
        tbl_62 = 0.05 * jax.random.normal(jax.random.fold_in(_tk, 500 + 62), (1000, 16), jnp.float32)
        tbl_63 = 0.05 * jax.random.normal(jax.random.fold_in(_tk, 500 + 63), (1000, 16), jnp.float32)
        _rk = jax.random.fold_in(_tk, 7)
        W_top1 = 0.05 * jax.random.normal(jax.random.fold_in(_tk, 801), (400, 512), jnp.float32)
        W_top2 = 0.0441942 * jax.random.normal(jax.random.fold_in(_tk, 802), (512, 256), jnp.float32)
        W_top3 = 0.0625 * jax.random.normal(jax.random.fold_in(_tk, 803), (256, 1), jnp.float32)
        b_top1 = jnp.zeros((512,), jnp.float32)
        b_top2 = jnp.zeros((256,), jnp.float32)
        return (dense_ctx, ids, tbl_0, tbl_1, tbl_2, tbl_3, tbl_4, tbl_5, tbl_6, tbl_7, tbl_8, tbl_9, tbl_10, tbl_11, tbl_12, tbl_13, tbl_14, tbl_15, tbl_16, tbl_17, tbl_18, tbl_19, tbl_20, tbl_21, tbl_22, tbl_23, tbl_24, tbl_25, tbl_26, tbl_27, tbl_28, tbl_29, tbl_30, tbl_31, tbl_32, tbl_33, tbl_34, tbl_35, tbl_36, tbl_37, tbl_38, tbl_39, tbl_40, tbl_41, tbl_42, tbl_43, tbl_44, tbl_45, tbl_46, tbl_47, tbl_48, tbl_49, tbl_50, tbl_51, tbl_52, tbl_53, tbl_54, tbl_55, tbl_56, tbl_57, tbl_58, tbl_59, tbl_60, tbl_61, tbl_62, tbl_63, W_top1, b_top1, W_top2, b_top2, W_top3)
    dense_ctx, ids, tbl_0, tbl_1, tbl_2, tbl_3, tbl_4, tbl_5, tbl_6, tbl_7, tbl_8, tbl_9, tbl_10, tbl_11, tbl_12, tbl_13, tbl_14, tbl_15, tbl_16, tbl_17, tbl_18, tbl_19, tbl_20, tbl_21, tbl_22, tbl_23, tbl_24, tbl_25, tbl_26, tbl_27, tbl_28, tbl_29, tbl_30, tbl_31, tbl_32, tbl_33, tbl_34, tbl_35, tbl_36, tbl_37, tbl_38, tbl_39, tbl_40, tbl_41, tbl_42, tbl_43, tbl_44, tbl_45, tbl_46, tbl_47, tbl_48, tbl_49, tbl_50, tbl_51, tbl_52, tbl_53, tbl_54, tbl_55, tbl_56, tbl_57, tbl_58, tbl_59, tbl_60, tbl_61, tbl_62, tbl_63, W_top1, b_top1, W_top2, b_top2, W_top3 = _rec_inputs()

    def _L0_rec_setup():
        import jax, jax.numpy as jnp
        import numpy as np
        BATCH, FIELDS, EMBED = (256, 64, 16)
        LAYERS = [128, 128, 128]
        key = jax.random.key(seed)
        ks = jax.random.split(key, 7)
        inp = {'input': jax.random.normal(ks[0], (BATCH, FIELDS, EMBED), dtype=jnp.float32)}
        in_ch = [FIELDS * FIELDS, FIELDS * LAYERS[0], FIELDS * LAYERS[1]]
        for i, (cin, cout) in enumerate(zip(in_ch, LAYERS)):
            scale = 1.0 / np.sqrt(cin)
            inp[f'W{i}'] = jax.random.uniform(ks[1 + 2 * i], (cout, cin), jnp.float32, -scale, scale)
            inp[f'b{i}'] = jax.random.uniform(ks[2 + 2 * i], (cout,), jnp.float32, -scale, scale)
        return inp
    _L0_rec_all = _L0_rec_setup()
    _L0_rec_in = {k: v for k, v in _L0_rec_all.items() if k in ('W0', 'b0', 'W1', 'b1', 'W2', 'b2')}
    del _L0_rec_all
    return {'dense_ctx': dense_ctx, 'ids': ids, 'tbl_0': tbl_0, 'tbl_1': tbl_1, 'tbl_2': tbl_2, 'tbl_3': tbl_3, 'tbl_4': tbl_4, 'tbl_5': tbl_5, 'tbl_6': tbl_6, 'tbl_7': tbl_7, 'tbl_8': tbl_8, 'tbl_9': tbl_9, 'tbl_10': tbl_10, 'tbl_11': tbl_11, 'tbl_12': tbl_12, 'tbl_13': tbl_13, 'tbl_14': tbl_14, 'tbl_15': tbl_15, 'tbl_16': tbl_16, 'tbl_17': tbl_17, 'tbl_18': tbl_18, 'tbl_19': tbl_19, 'tbl_20': tbl_20, 'tbl_21': tbl_21, 'tbl_22': tbl_22, 'tbl_23': tbl_23, 'tbl_24': tbl_24, 'tbl_25': tbl_25, 'tbl_26': tbl_26, 'tbl_27': tbl_27, 'tbl_28': tbl_28, 'tbl_29': tbl_29, 'tbl_30': tbl_30, 'tbl_31': tbl_31, 'tbl_32': tbl_32, 'tbl_33': tbl_33, 'tbl_34': tbl_34, 'tbl_35': tbl_35, 'tbl_36': tbl_36, 'tbl_37': tbl_37, 'tbl_38': tbl_38, 'tbl_39': tbl_39, 'tbl_40': tbl_40, 'tbl_41': tbl_41, 'tbl_42': tbl_42, 'tbl_43': tbl_43, 'tbl_44': tbl_44, 'tbl_45': tbl_45, 'tbl_46': tbl_46, 'tbl_47': tbl_47, 'tbl_48': tbl_48, 'tbl_49': tbl_49, 'tbl_50': tbl_50, 'tbl_51': tbl_51, 'tbl_52': tbl_52, 'tbl_53': tbl_53, 'tbl_54': tbl_54, 'tbl_55': tbl_55, 'tbl_56': tbl_56, 'tbl_57': tbl_57, 'tbl_58': tbl_58, 'tbl_59': tbl_59, 'tbl_60': tbl_60, 'tbl_61': tbl_61, 'tbl_62': tbl_62, 'tbl_63': tbl_63, 'W_top1': W_top1, 'b_top1': b_top1, 'W_top2': W_top2, 'b_top2': b_top2, 'W_top3': W_top3, 'L0_rec_W0': _L0_rec_in['W0'], 'L0_rec_b0': _L0_rec_in['b0'], 'L0_rec_W1': _L0_rec_in['W1'], 'L0_rec_b1': _L0_rec_in['b1'], 'L0_rec_W2': _L0_rec_in['W2'], 'L0_rec_b2': _L0_rec_in['b2']}

def reference(dense_ctx, ids, tbl_0, tbl_1, tbl_2, tbl_3, tbl_4, tbl_5, tbl_6, tbl_7, tbl_8, tbl_9, tbl_10, tbl_11, tbl_12, tbl_13, tbl_14, tbl_15, tbl_16, tbl_17, tbl_18, tbl_19, tbl_20, tbl_21, tbl_22, tbl_23, tbl_24, tbl_25, tbl_26, tbl_27, tbl_28, tbl_29, tbl_30, tbl_31, tbl_32, tbl_33, tbl_34, tbl_35, tbl_36, tbl_37, tbl_38, tbl_39, tbl_40, tbl_41, tbl_42, tbl_43, tbl_44, tbl_45, tbl_46, tbl_47, tbl_48, tbl_49, tbl_50, tbl_51, tbl_52, tbl_53, tbl_54, tbl_55, tbl_56, tbl_57, tbl_58, tbl_59, tbl_60, tbl_61, tbl_62, tbl_63, W_top1, b_top1, W_top2, b_top2, W_top3, L0_rec_W0, L0_rec_b0, L0_rec_W1, L0_rec_b1, L0_rec_W2, L0_rec_b2):
    import jax
    import jax.numpy as jnp

    def _L0_rec_ref(input, W0, b0, W1, b1, W2, b2):
        import jax, jax.numpy as jnp
        import numpy as np
        BATCH, FIELDS, EMBED = (256, 64, 16)
        LAYERS = [128, 128, 128]
        params = [(W0, b0), (W1, b1), (W2, b2)]
        x_vec = input
        outs = []
        for W, b in params:
            z = jnp.einsum('bhd,bfd->bhfd', x_vec, input)
            B, h, f, d = z.shape
            z = z.reshape(B, h * f, d)
            x_vec = jnp.einsum('oc,bcd->bod', W, z) + b[None, :, None]
            outs.append(x_vec.sum(axis=2))
        return jnp.concatenate(outs, axis=1)
    e = jnp.stack([tbl_0[ids[:, 0]], tbl_1[ids[:, 1]], tbl_2[ids[:, 2]], tbl_3[ids[:, 3]], tbl_4[ids[:, 4]], tbl_5[ids[:, 5]], tbl_6[ids[:, 6]], tbl_7[ids[:, 7]], tbl_8[ids[:, 8]], tbl_9[ids[:, 9]], tbl_10[ids[:, 10]], tbl_11[ids[:, 11]], tbl_12[ids[:, 12]], tbl_13[ids[:, 13]], tbl_14[ids[:, 14]], tbl_15[ids[:, 15]], tbl_16[ids[:, 16]], tbl_17[ids[:, 17]], tbl_18[ids[:, 18]], tbl_19[ids[:, 19]], tbl_20[ids[:, 20]], tbl_21[ids[:, 21]], tbl_22[ids[:, 22]], tbl_23[ids[:, 23]], tbl_24[ids[:, 24]], tbl_25[ids[:, 25]], tbl_26[ids[:, 26]], tbl_27[ids[:, 27]], tbl_28[ids[:, 28]], tbl_29[ids[:, 29]], tbl_30[ids[:, 30]], tbl_31[ids[:, 31]], tbl_32[ids[:, 32]], tbl_33[ids[:, 33]], tbl_34[ids[:, 34]], tbl_35[ids[:, 35]], tbl_36[ids[:, 36]], tbl_37[ids[:, 37]], tbl_38[ids[:, 38]], tbl_39[ids[:, 39]], tbl_40[ids[:, 40]], tbl_41[ids[:, 41]], tbl_42[ids[:, 42]], tbl_43[ids[:, 43]], tbl_44[ids[:, 44]], tbl_45[ids[:, 45]], tbl_46[ids[:, 46]], tbl_47[ids[:, 47]], tbl_48[ids[:, 48]], tbl_49[ids[:, 49]], tbl_50[ids[:, 50]], tbl_51[ids[:, 51]], tbl_52[ids[:, 52]], tbl_53[ids[:, 53]], tbl_54[ids[:, 54]], tbl_55[ids[:, 55]], tbl_56[ids[:, 56]], tbl_57[ids[:, 57]], tbl_58[ids[:, 58]], tbl_59[ids[:, 59]], tbl_60[ids[:, 60]], tbl_61[ids[:, 61]], tbl_62[ids[:, 62]], tbl_63[ids[:, 63]]], axis=1)
    z = _L0_rec_ref(e, L0_rec_W0, L0_rec_b0, L0_rec_W1, L0_rec_b1, L0_rec_W2, L0_rec_b2)
    z = z.reshape(z.shape[0], -1)
    h = jnp.concatenate([z, dense_ctx], axis=1)
    h = jnp.maximum(h @ W_top1 + b_top1, 0.0)
    h = jnp.maximum(h @ W_top2 + b_top2, 0.0)
    y = h @ W_top3
    return y

_drawn_inputs = setup_inputs


def setup_inputs(seed=0):
    import zlib

    import numpy as np

    out = dict(_drawn_inputs(seed))
    spreads = {'b_top1': (0.0, 0.1), 'b_top2': (0.0, 0.1)}
    factors = {'tbl_0': 8.0,
     'tbl_1': 8.0,
     'tbl_2': 8.0,
     'tbl_3': 8.0,
     'tbl_4': 8.0,
     'tbl_5': 8.0,
     'tbl_6': 8.0,
     'tbl_7': 8.0,
     'tbl_8': 8.0,
     'tbl_9': 8.0,
     'tbl_10': 8.0,
     'tbl_11': 8.0,
     'tbl_12': 8.0,
     'tbl_13': 8.0,
     'tbl_14': 8.0,
     'tbl_15': 8.0,
     'tbl_16': 8.0,
     'tbl_17': 8.0,
     'tbl_18': 8.0,
     'tbl_19': 8.0,
     'tbl_20': 8.0,
     'tbl_21': 8.0,
     'tbl_22': 8.0,
     'tbl_23': 8.0,
     'tbl_24': 8.0,
     'tbl_25': 8.0,
     'tbl_26': 8.0,
     'tbl_27': 8.0,
     'tbl_28': 8.0,
     'tbl_29': 8.0,
     'tbl_30': 8.0,
     'tbl_31': 8.0,
     'tbl_32': 8.0,
     'tbl_33': 8.0,
     'tbl_34': 8.0,
     'tbl_35': 8.0,
     'tbl_36': 8.0,
     'tbl_37': 8.0,
     'tbl_38': 8.0,
     'tbl_39': 8.0,
     'tbl_40': 8.0,
     'tbl_41': 8.0,
     'tbl_42': 8.0,
     'tbl_43': 8.0,
     'tbl_44': 8.0,
     'tbl_45': 8.0,
     'tbl_46': 8.0,
     'tbl_47': 8.0,
     'tbl_48': 8.0,
     'tbl_49': 8.0,
     'tbl_50': 8.0,
     'tbl_51': 8.0,
     'tbl_52': 8.0,
     'tbl_53': 8.0,
     'tbl_54': 8.0,
     'tbl_55': 8.0,
     'tbl_56': 8.0,
     'tbl_57': 8.0,
     'tbl_58': 8.0,
     'tbl_59': 8.0,
     'tbl_60': 8.0,
     'tbl_61': 8.0,
     'tbl_62': 8.0,
     'tbl_63': 8.0,
     'L0_rec_W0': 2.692,
     'L0_rec_W1': 8.0,
     'L0_rec_W2': 8.0}
    for name, (base, spread) in spreads.items():
        noise = np.random.default_rng([zlib.crc32(name.encode()), seed]).standard_normal(out[name].shape)
        drawn = base * np.exp(spread * noise) if base else spread * noise
        out[name] = jnp.asarray(drawn.astype(out[name].dtype))
    for name, factor in factors.items():
        out[name] = (out[name] * factor).astype(out[name].dtype)
    return out
```

```python
import concourse.bass as bass
from concourse import mybir
from contextlib import ExitStack

F32 = mybir.dt.float32
I32 = mybir.dt.int32
ALU = mybir.AluOpType
ACT = mybir.ActivationFunctionType
AX_X = mybir.AxisListType.X

P = 128
BATCH, FIELDS, DIM, DENSE = 512, 64, 16, 16
H = 128
TOP1, TOP2 = 512, 256
CB = 32
NC = CB * DIM
NCHUNK = BATCH // CB
GC = 4
NG = NCHUNK // GC
GB = GC * CB
QT = 4
SHIFTS = FIELDS // 2 + 1
T0 = (SHIFTS + 1) // 2
R_ITEMS = 1 + (T0 - 1) // QT
Q_ITEMS = FIELDS * H // P // QT
ZRING = 3
GPQ = P // DIM
NQ = NC // P
W2P = 8
W2F = FIELDS // W2P
W2RING = 4
GATHERS = CB // 2
AHEAD = 2

FULL = ([("q", i) for i in range(3)] + [("r", 0)] + [("q", i) for i in range(3, 6)] + [("r", 1)]
        + [("q", i) for i in range(6, 11)] + [("r", 2)] + [("q", i) for i in range(11, 16)]
        + [("r", 3), ("r", 4)])
SHORT = [("q", i) for i in range(16)]
HEAD_ITEMS = AHEAD * R_ITEMS
X0T_AFTER = ("q", 11)
BD_AFTER = ("q", 13)
SUM1_AFTER = ("q", 1)


def body_items(last, c):
    return SHORT if last and c >= GC - AHEAD else FULL


def item_number(g, last, c, item):
    before = sum(len(body_items(last, e)) for e in range(c))
    return HEAD_ITEMS + GC * len(FULL) * g + before + body_items(last, c).index(item)


def r_tiles(r):
    return [T0 - 1] if r == 0 else list(range(QT * (r - 1), QT * r))


def slot_of(number):
    return number % ZRING


def cin_tower(nc, ids, table, dense_t, consts, params, w0a, w0b, w1, w2, wt1, wt2, out):
    ctx = ExitStack()
    with ctx:
        def sb(name, shape, dt=F32):
            return ctx.enter_context(nc.sbuf_tensor(name, shape, dt))

        def pb(name, shape):
            return ctx.enter_context(nc.psum_tensor(name, shape, F32))

        def sem(name):
            return ctx.enter_context(nc.semaphore(name))

        x0_dram = nc.dram_tensor("x0_scratch", (GC, 2 * FIELDS, NC), F32, kind="Internal").ap()
        x1_dram = nc.dram_tensor("x1_scratch", (2, H, NC), F32, kind="Internal").ap()

        const_sb = sb("const_sb", [P, GPQ + P + 2])
        mask = const_sb[:, 0:GPQ]
        ident = const_sb[:, GPQ:GPQ + P]
        vmax = const_sb[:, GPQ + P:GPQ + P + 1]
        voff = const_sb[:, GPQ + P + 1:GPQ + P + 2]
        rows_sb = sb("rows_sb", [P, NCHUNK * GATHERS], I32)
        rows_chunk = sb("rows_chunk", [P, GC, GATHERS], I32)
        xg = sb("xg", [P, GC, GATHERS * DIM])
        w0_sb = sb("w0_sb", [P, T0, H])
        w1_sb = sb("w1_sb", [P, Q_ITEMS * QT, H])
        w2_sb = sb("w2_sb", [P, W2RING, W2F, H])
        xi = sb("xi", [P, 2, NC])
        xs = sb("xs", [P, 2, QT, NC])
        xv = sb("xv", [P, 8, NC])
        xu = sb("xu", [P, 2, 8, NC])
        carrier = sb("carrier", [P, 1])
        z = sb("z", [P, ZRING, QT, NC])
        x1_sb = sb("x1_sb", [P, NC])
        x2_sb = sb("x2_sb", [P, NC])
        x2t_sb = sb("x2t_sb", [P, NC])
        x0bd = sb("x0bd", [P, NQ, GPQ, FIELDS])
        g_sb = sb("g_sb", [P, FIELDS, GB])
        sums = sb("sums", [P, 3, BATCH])
        M1, M2 = TOP1 // P, TOP2 // P
        params_sb = sb("params_sb", [P, 3 + M1 + 2 * M2])
        bias = params_sb[:, 0:3]
        bt_sb = params_sb[:, 3:3 + M1 + M2]
        wt3_sb = params_sb[:, 3 + M1 + M2:3 + M1 + 2 * M2]
        b2_sum = sb("b2_sum", [P, 1])
        y_sb = x2_sb[0:1, :]
        ids_sb = x2t_sb[:, 0:NCHUNK * GATHERS].bitcast(I32)
        w0b_sb = g_sb[:, 0:(T0 - 1), :]
        wt1_sb = xu[:, 0, 0:3 * TOP1 // NC, :]
        wt1d_sb = xu[0:DENSE, 0, 3, :]
        wt2_sb = xu[:, 0, 4:6, :].rearrange("p a n -> p (a n)").rearrange("p (k m) -> p k m", m=TOP2)
        dense_sb = xu[0:DENSE, 0, 6, :]
        h1_sb = xs[:, 0, :, :]
        h2_sb = xs[:, 1, 0:2, :]

        acc0 = pb("acc0", [P, NC])
        acc1 = [pb(f"acc1_{i}", [P, NC]) for i in range(2)]
        x2t_ps = pb("x2t_ps", [P, NC])
        x0t_ps = pb("x0t_ps", [P, 2, P])
        g_ps = [pb(f"g_ps_{i}", [P, GPQ * FIELDS]) for i in range(2)]
        x3_ps = pb("x3_ps", [P, GB])
        h_ps = [acc1[0], acc1[1], g_ps[0], g_ps[1]]

        const_loaded = sem("const_loaded")
        ids_loaded = sem("ids_loaded")
        rows_ready = sem("rows_ready")
        rows_copied = sem("rows_copied")
        gathered = [sem(f"gathered_{i}") for i in range(GC)]
        x0_stored = [sem(f"x0_stored_{i}") for i in range(GC)]
        w0_loaded = sem("w0_loaded")
        w0b_loaded = sem("w0b_loaded")
        w0_ready = sem("w0_ready")
        w1_loaded = [sem(f"w1_loaded_{i}") for i in range(2)]
        w2_loaded = [sem(f"w2_loaded_{i}") for i in range(W2RING)]
        bias_loaded = sem("bias_loaded")
        bias_ready = sem("bias_ready")
        xi_loaded = [sem(f"xi_loaded_{i}") for i in range(2)]
        xs_loaded = [sem(f"xs_loaded_{i}") for i in range(2)]
        xv_loaded = [sem(f"xv_loaded_{i}") for i in range(2)]
        xu_loaded = [sem(f"xu_loaded_{i}") for i in range(2)]
        z_ready = sem("z_ready")
        z_used = sem("z_used")
        x1_ready = sem("x1_ready")
        x1_stored = [sem(f"x1_stored_{i}") for i in range(2)]
        x1_summed = sem("x1_summed")
        x2_ready = sem("x2_ready")
        x2_summed = sem("x2_summed")
        x2t_done = sem("x2t_done")
        x2t_ready = sem("x2t_ready")
        x0t_done = sem("x0t_done")
        x0bd_ready = sem("x0bd_ready")
        g_done = sem("g_done")
        g_ready = sem("g_ready")
        x3_piece = sem("x3_piece")
        x3_ready = sem("x3_ready")
        top_loaded = sem("top_loaded")
        h_done = sem("h_done")
        h_ready = sem("h_ready")
        y_stored = sem("y_stored")

        block = ctx.enter_context(nc.Block())

        def layer1_end(g, last, c):
            return item_number(g, last, c, ("q", 15)) + 1

        def run_groups(eng, group):
            with eng.Fori(0, NG - 1) as g:
                group(g, False)
            group(NG - 1, True)

        @block.sync
        def _(sp):
            sp.dma_start(ids_sb[:], ids).then_inc(ids_loaded, 16)
            sp.dma_start(const_sb[:], consts).then_inc(const_loaded, 16)

            def store_x0(uses, s):
                sp.wait_ge(gathered[s], 16 * GATHERS * uses)
                for half in range(2):
                    for copy in range(2):
                        sp.dma_start(x0_dram[s, copy * FIELDS:(copy + 1) * FIELDS, half * NC // 2:(half + 1) * NC // 2],
                                     xg[half * FIELDS:(half + 1) * FIELDS, s, :]).then_inc(x0_stored[s], 16)

            def load_xi(s, par):
                for s2 in range(2):
                    sp.dma_start(xi[s2 * FIELDS:(s2 + 1) * FIELDS, par, :],
                                 x0_dram[s, 0:FIELDS, :]).then_inc(xi_loaded[par], 16)

            def load_xs(s, r, slot):
                tiles = r_tiles(r)
                for s2 in range(1 if r == 0 else 2):
                    first = s2 + 2 * tiles[0]
                    src = x0_dram[s, first:first + FIELDS, :]
                    src = bass.AP(src.tensor, src.offset, [[NC, FIELDS], [2 * NC, len(tiles)], [1, NC]])
                    sp.dma_start(xs[s2 * FIELDS:(s2 + 1) * FIELDS, slot, 0:len(tiles), :], src)\
                        .then_inc(xs_loaded[slot], 16 if r else 32)

            def load_xv(s, half):
                src = x0_dram[s, 0:FIELDS, :].rearrange("(c j) n -> c (j n)", j=8)
                src = src[:, half * 4 * NC:(half + 1) * 4 * NC].unsqueeze(0).to_broadcast([16, 8, 4 * NC])
                sp.dma_start(xv[:, half * 4:half * 4 + 4, :].rearrange("p j n -> p (j n)"), src)\
                    .then_inc(xv_loaded[half], 16)

            def load_xu(par):
                src = x1_dram[par, :, :].rearrange("(a i) n -> a (i n)", i=8)
                src = src.unsqueeze(1).to_broadcast([16, 8, 8 * NC])
                sp.dma_start(xu[:, par, :, :].rearrange("p j n -> p (j n)"), src).then_inc(xu_loaded[par], 16)

            store_x0(1, 0)
            sp.wait_ge(x0_stored[0], 64)
            load_xi(0, 0)
            load_xs(0, 0, 0)
            load_xs(0, 1, 1)
            for r in range(2, R_ITEMS):
                sp.wait_ge(z_ready, r - 1)
                load_xs(0, r, r % 2)
                if r == 3:
                    load_xv(0, 0)
            store_x0(1, 1)
            sp.wait_ge(x0_stored[1], 64)
            load_xi(1, 1)
            for r in range(R_ITEMS):
                sp.wait_ge(z_ready, R_ITEMS + r - 1)
                load_xs(1, r, (R_ITEMS + r) % 2)
            sp.wait_ge(x1_stored[0], 16)
            load_xu(0)
            store_x0(1, 2)

            def group(g, last):
                for c in range(GC):
                    items = body_items(last, c)
                    par = c % 2
                    sp.wait_ge(z_ready, item_number(g, last, c, ("q", 0)))
                    load_xv(c, 1)
                    if not (last and c == GC - 1):
                        sp.wait_ge(x1_stored[1 - par], 16 * (GC // 2) * g + 16 * (1 + (c + 1) // 2))
                        load_xu(1 - par)
                    nxt = (c + AHEAD) % GC
                    if items is FULL:
                        sp.wait_ge(x0_stored[nxt], 64 * g + 64 * (1 + (c + AHEAD) // GC))
                        load_xi(nxt, par)
                        for r in range(R_ITEMS - 1):
                            n = R_ITEMS * (c + AHEAD) + r
                            if r >= 2:
                                sp.wait_ge(z_ready, item_number(g, last, c, ("r", r - 2)) + 1)
                            load_xs(nxt, r, n % 2)
                    if not (last and c == GC - 1):
                        sp.wait_ge(z_ready, item_number(g, last, c, ("q", 7)) + 1)
                        load_xv((c + 1) % GC, 0)
                    if items is FULL:
                        sp.wait_ge(z_ready, item_number(g, last, c, ("r", 2)) + 1)
                        load_xs(nxt, 4, (R_ITEMS * (c + AHEAD) + 4) % 2)
                    if not (last and c >= 1):
                        e = c + 3
                        store_x0(g + 1 + e // GC, e % GC)
                    if c == GC - 1:
                        for p in range(W2P):
                            n = W2P * g + p
                            slot = p % W2RING
                            if p >= W2RING:
                                sp.wait_ge(x3_piece, n - W2RING + 1)
                            sp.dma_start(w2_sb[:, slot, :, :], w2[:, p * W2F:(p + 1) * W2F, :])\
                                .then_inc(w2_loaded[slot], 16)

            run_groups(sp, group)

            sp.wait_ge(z_ready, layer1_end(NG - 1, True, GC - 2))
            sp.dma_start(wt1_sb, wt1[0:3 * H, :].rearrange("(k p) m -> p k m", p=H)).then_inc(top_loaded, 16)
            sp.dma_start(wt1d_sb, wt1[3 * H:3 * H + DENSE, :]).then_inc(top_loaded, 16)
            sp.dma_start(wt2_sb, wt2.rearrange("(k p) m -> p k m", p=P)).then_inc(top_loaded, 16)
            sp.dma_start(dense_sb, dense_t).then_inc(top_loaded, 16)
            sp.wait_ge(h_ready, TOP1 // P + TOP2 // P + 1)
            sp.dma_start(out.rearrange("b a -> a b"), y_sb[:]).then_inc(y_stored, 16)
            sp.wait_ge(y_stored, 16)

        @block.gpsimd
        def _(pool):
            pool.wait_ge(rows_ready, 1)

            def gather(chunk, copies, s):
                nc.gpsimd.tensor_copy(rows_chunk[:, s, :], rows_sb[:, bass.ds(GATHERS * chunk, GATHERS)])\
                    .then_inc(rows_copied, 1)
                pool.wait_ge(rows_copied, copies)
                nc.gpsimd.tensor_tensor(carrier[:], vmax, voff, ALU.add)
                for j in range(GATHERS):
                    nc.gpsimd.indirect_dma_start(
                        out=xg[:, s, j * DIM:(j + 1) * DIM], out_offset=None, in_=table,
                        in_offset=bass.IndirectOffsetOnAxis(ap=rows_chunk[:, s, j:j + 1], axis=0))\
                        .then_inc(gathered[s], 16)

            for c in range(GC):
                gather(c, c + 1, c)

            with pool.Fori(0, NG - 1) as g:
                for c in range(GC):
                    pool.wait_ge(x0t_done, GC * g + c + 1)
                    gather(GC * g + c + GC, GC * g + c + GC + 1, c)

        @block.scalar
        def _(act):
            act.dma_start(w0_sb[:], w0a).then_inc(w0_loaded, 16)
            act.dma_start(w0b_sb, w0b).then_inc(w0b_loaded, 16)
            act.dma_start(params_sb[:], params).then_inc(bias_loaded, 16)
            for half in range(2):
                h = Q_ITEMS * QT // 2
                act.dma_start(w1_sb[:, half * h:(half + 1) * h, :], w1[:, half * h:(half + 1) * h, :])\
                    .then_inc(w1_loaded[half], 16)
            act.wait_ge(bias_loaded, 16)
            nc.scalar.mul(b2_sum[:], bias[:, 2:3], float(DIM)).then_inc(bias_ready, 1)

            def finish_x1(chunks, used, par, stored):
                act.wait_ge(z_used, used)
                if stored is not None:
                    act.wait_ge(x1_stored[1 - par], stored)
                    act.wait_ge(x1_summed, chunks - 1)
                nc.scalar.activation(x1_sb[:], acc0[:], ACT.Identity, bias=bias[:, 0:1])\
                    .then_inc(x1_ready, 1)
                act.wait_ge(x1_ready, chunks)
                act.dma_start(x1_dram[par, :, :], x1_sb[:]).then_inc(x1_stored[par], 16)

            finish_x1(1, R_ITEMS, 0, None)
            finish_x1(2, 2 * R_ITEMS, 1, 16)
            act.wait_ge(bias_ready, 1)

            def group(g, last):
                for c in range(GC):
                    k = GC * g + c
                    par = c % 2
                    act.wait_ge(z_used, layer1_end(g, last, c))
                    nc.scalar.activation(x2_sb[:], acc1[par][:], ACT.Identity, bias=bias[:, 1:2])\
                        .then_inc(x2_ready, 1)
                    act.wait_ge(x2t_done, k + 1)
                    nc.scalar.activation(x2t_sb[:], x2t_ps[:], ACT.Copy).then_inc(x2t_ready, 1)
                    if body_items(last, c) is FULL:
                        finish_x1(k + AHEAD + 1, item_number(g, last, c, ("r", R_ITEMS - 1)) + 1, par,
                                  16 * (GC // 2) * g + 16 * (1 + (c + 1) // 2))
                    for q in range(NQ):
                        act.wait_ge(g_done, NQ * k + q + 1)
                        b = c * CB + q * GPQ
                        nc.scalar.activation(g_sb[:, :, b:b + GPQ].rearrange("p f b -> p b f"),
                                             g_ps[q % 2][:].rearrange("p (b f) -> p b f", f=FIELDS),
                                             ACT.Copy).then_inc(g_ready, 1)
                act.wait_ge(x3_piece, W2P * g + W2P)
                nc.scalar.activation(sums[:, 2, bass.ds(GB * g, GB)], x3_ps[:], ACT.Identity,
                                     bias=b2_sum[:]).then_inc(x3_ready, 1)

            run_groups(act, group)

            for m in range(TOP1 // P):
                act.wait_ge(h_done, m + 1)
                nc.scalar.activation(h1_sb[:, m, :], h_ps[m][:], ACT.Relu, bias=bt_sb[:, m:m + 1])\
                    .then_inc(h_ready, 1)
            for m in range(TOP2 // P):
                act.wait_ge(h_done, TOP1 // P + m + 1)
                nc.scalar.activation(h2_sb[:, m, :], h_ps[m][:], ACT.Relu, bias=bt_sb[:, 4 + m:5 + m])\
                    .then_inc(h_ready, 1)
            act.wait_ge(h_done, TOP1 // P + TOP2 // P + 1)
            nc.scalar.activation(y_sb[:], h_ps[2][0:1, :], ACT.Copy).then_inc(h_ready, 1)

        @block.vector
        def _(dve):
            dve.wait_ge(ids_loaded, 16)
            dve.wait_ge(const_loaded, 16)
            nc.vector.tensor_scalar(rows_sb[:], ids_sb[:], vmax, voff, ALU.min, ALU.add).then_inc(rows_ready, 1)
            dve.wait_ge(w0_loaded, 16)
            dve.wait_ge(w0b_loaded, 16)
            nc.vector.tensor_tensor(w0_sb[FIELDS:P, 0, :], w0_sb[FIELDS:P, 0, :], w0b_sb[FIELDS:P, 0, :], ALU.add)\
                .then_inc(w0_ready, 1)
            nc.vector.tensor_tensor(w0_sb[:, 1:T0 - 1, :], w0_sb[:, 1:T0 - 1, :], w0b_sb[:, 1:T0 - 1, :], ALU.add)\
                .then_inc(w0_ready, 1)

            def free_z(number):
                if not isinstance(number, int) or number >= ZRING:
                    dve.wait_ge(z_used, number - ZRING + 1)

            def make_r(number, zs, slot, nth, par, r):
                dve.wait_ge(xs_loaded[slot], nth)
                free_z(number)
                tiles = len(r_tiles(r))
                rows = FIELDS if r == 0 else P
                nc.vector.tensor_tensor(z[0:rows, zs, 0:tiles, :],
                                        xi[0:rows, par, :].unsqueeze(1).to_broadcast([rows, tiles, NC]),
                                        xs[0:rows, slot, 0:tiles, :], ALU.mult).then_inc(z_ready, 1)

            def make_q(number, zs, par, q):
                free_z(number)
                half, i = q // 8, q % 8
                nc.vector.tensor_tensor(z[:, zs, :, :],
                                        xu[:, par, i, :].unsqueeze(1).to_broadcast([P, QT, NC]),
                                        xv[:, 4 * half:4 * half + 4, :], ALU.mult).then_inc(z_ready, 1)

            def sum_x1(k):
                dve.wait_ge(x1_ready, k + 1)
                nc.vector.tensor_reduce(sums[:, 0, bass.ds(CB * k, CB)],
                                        x1_sb[:].rearrange("p (b d) -> p b d", d=DIM),
                                        AX_X, ALU.add).then_inc(x1_summed, 1)

            for c in range(AHEAD):
                dve.wait_ge(xi_loaded[c], 32)
                for r in range(R_ITEMS):
                    n = R_ITEMS * c + r
                    make_r(n, n % ZRING, n % 2, 32 * (n // 2 + 1), c, r)
            sum_x1(0)

            def group(g, last):
                for c in range(GC):
                    k = GC * g + c
                    par = c % 2
                    for kind, i in body_items(last, c):
                        number = item_number(g, last, c, (kind, i))
                        zs = item_number(0, last, c, (kind, i)) % ZRING
                        if kind == "q":
                            if i == 0:
                                dve.wait_ge(xu_loaded[par], 16 * (GC // 2) * g + 16 * (1 + c // 2))
                                dve.wait_ge(xv_loaded[0], 16 * GC * g + 16 * (c + 1))
                            if i == 8:
                                dve.wait_ge(xv_loaded[1], 16 * GC * g + 16 * (c + 1))
                            make_q(number, zs, par, i)
                        else:
                            if i == 0:
                                dve.wait_ge(xi_loaded[par], 32 * (GC // 2) * g + 32 * (c // 2 + 2))
                            n = R_ITEMS * (c + AHEAD) + i
                            make_r(number, zs, n % 2, 32 * (R_ITEMS * GC // 2) * g + 32 * (n // 2 + 1), par, i)
                        if (kind, i) == SUM1_AFTER and not (last and c == GC - 1):
                            sum_x1(k + 1)
                        if (kind, i) == BD_AFTER:
                            dve.wait_ge(x0t_done, k + 1)
                            for half in range(2):
                                nc.vector.tensor_tensor(
                                    x0bd[:, 2 * half:2 * half + 2, :, :],
                                    x0t_ps[:, :, half * FIELDS:(half + 1) * FIELDS].unsqueeze(2)
                                    .to_broadcast([P, 2, GPQ, FIELDS]),
                                    mask.unsqueeze(1).unsqueeze(3).to_broadcast([P, 2, GPQ, FIELDS]),
                                    ALU.mult).then_inc(x0bd_ready, 1)
                    dve.wait_ge(x2_ready, k + 1)
                    nc.vector.tensor_reduce(sums[:, 1, bass.ds(CB * k, CB)],
                                            x2_sb[:].rearrange("p (b d) -> p b d", d=DIM),
                                            AX_X, ALU.add).then_inc(x2_summed, 1)

            run_groups(dve, group)

        @block.tensor
        def _(pe):
            pe.wait_ge(w0_ready, 2)

            def use_r(number, zs, r):
                pe.wait_ge(z_ready, number + 1)
                tiles = r_tiles(r)
                for n, t in enumerate(tiles):
                    rows = FIELDS if r == 0 else P
                    mm = nc.tensor.matmul(acc0[:], w0_sb[0:rows, t, :], z[0:rows, zs, n, :],
                                          start=(r == 0), stop=(r == R_ITEMS - 1 and n == len(tiles) - 1))
                mm.then_inc(z_used, 1)

            def use_q(number, zs, par, q):
                pe.wait_ge(z_ready, number + 1)
                for n in range(QT):
                    mm = nc.tensor.matmul(acc1[par][:], w1_sb[:, QT * q + n, :], z[:, zs, n, :],
                                          start=(q == 0 and n == 0), stop=(q == Q_ITEMS - 1 and n == QT - 1))
                mm.then_inc(z_used, 1)

            for c in range(AHEAD):
                if c:
                    pe.wait_ge(x1_ready, c)
                for r in range(R_ITEMS):
                    n = R_ITEMS * c + r
                    use_r(n, n % ZRING, r)
            for half in range(2):
                pe.wait_ge(w1_loaded[half], 16)
            pe.wait_ge(const_loaded, 16)

            def group(g, last):
                for c in range(GC):
                    k = GC * g + c
                    par = c % 2
                    for kind, i in body_items(last, c) + [("end", 0)]:
                        if kind == "q":
                            number = item_number(g, last, c, (kind, i))
                            use_q(number, item_number(0, last, c, (kind, i)) % ZRING, par, i)
                        elif kind == "r":
                            if i == 0:
                                pe.wait_ge(x1_ready, k + AHEAD)
                            number = item_number(g, last, c, (kind, i))
                            use_r(number, item_number(0, last, c, (kind, i)) % ZRING, i)
                        if (kind, i) == X0T_AFTER:
                            pe.wait_ge(gathered[c], 16 * GATHERS * g + 16 * GATHERS)
                            for m in range(2):
                                mm = nc.tensor.transpose(x0t_ps[:, m, :], xg[:, c, m * P:(m + 1) * P], ident)
                            mm.then_inc(x0t_done, 1)
                        if (kind, i) == (("r", R_ITEMS - 2) if body_items(last, c) is FULL else ("q", 15)):
                            pe.wait_ge(x2_ready, k + 1)
                            for q in range(NQ):
                                mm = nc.tensor.transpose(x2t_ps[:, q * P:(q + 1) * P],
                                                         x2_sb[:, q * P:(q + 1) * P], ident)
                            mm.then_inc(x2t_done, 1)
                    pe.wait_ge(x2t_ready, k + 1)
                    pe.wait_ge(x0bd_ready, 2 * k + 2)
                    for q in range(NQ):
                        if q >= 2:
                            pe.wait_ge(g_ready, NQ * k + q - 1)
                        nc.tensor.matmul(g_ps[q % 2][:], x2t_sb[:, q * P:(q + 1) * P],
                                         x0bd[:, q, :, :].rearrange("p b f -> p (b f)"),
                                         start=True, stop=True).then_inc(g_done, 1)
                pe.wait_ge(g_ready, NQ * GC * g + NQ * GC)
                for p in range(W2P):
                    slot = p % W2RING
                    pe.wait_ge(w2_loaded[slot], 16 * (W2P // W2RING) * g + 16 * (p // W2RING + 1))
                    for n in range(W2F):
                        f = p * W2F + n
                        mm = nc.tensor.matmul(x3_ps[:], w2_sb[:, slot, n, :], g_sb[:, f, :],
                                              start=(f == 0), stop=(f == FIELDS - 1))
                    mm.then_inc(x3_piece, 1)

            run_groups(pe, group)

            pe.wait_ge(x3_ready, NG)
            pe.wait_ge(x1_summed, NCHUNK)
            pe.wait_ge(x2_summed, NCHUNK)
            pe.wait_ge(top_loaded, 64)
            for m in range(TOP1 // P):
                if m >= 2:
                    pe.wait_ge(g_ready, NQ * NCHUNK)
                for n in range(3):
                    nc.tensor.matmul(h_ps[m][:], wt1_sb[:, n, m * P:(m + 1) * P], sums[:, n, :],
                                     start=(n == 0), stop=False)
                nc.tensor.matmul(h_ps[m][:], wt1d_sb[:, m * P:(m + 1) * P], dense_sb,
                                 start=False, stop=True).then_inc(h_done, 1)
            pe.wait_ge(h_ready, TOP1 // P)
            for m in range(TOP2 // P):
                for n in range(TOP1 // P):
                    mm = nc.tensor.matmul(h_ps[m][:], wt2_sb[:, n, m * P:(m + 1) * P], h1_sb[:, n, :],
                                          start=(n == 0), stop=(n == TOP1 // P - 1))
                mm.then_inc(h_done, 1)
            pe.wait_ge(h_ready, TOP1 // P + TOP2 // P)
            for n in range(TOP2 // P):
                mm = nc.tensor.matmul(h_ps[2][0:1, :], wt3_sb[:, n:n + 1], h2_sb[:, n, :],
                                      start=(n == 0), stop=(n == TOP2 // P - 1))
            mm.then_inc(h_done, 1)


def kernel(**inputs):
    import numpy as _np
    import concourse.bacc as _bacc
    from concourse import mybir as _mybir
    from concourse.bass_utils import run_bass_kernel_spmd as _run

    tables = [_np.asarray(inputs[f"tbl_{f}"]) for f in range(FIELDS)]
    sizes = [t.shape[0] for t in tables]
    ids = _np.asarray(inputs["ids"]).reshape(NCHUNK, 2, GATHERS, FIELDS)
    w0 = _np.asarray(inputs["L0_rec_W0"]).reshape(H, FIELDS, FIELDS)
    w1 = _np.asarray(inputs["L0_rec_W1"]).reshape(H, 16, 8, 8, 2, 4)
    w2 = _np.asarray(inputs["L0_rec_W2"]).reshape(H, H, FIELDS)

    first = _np.tile(_np.arange(FIELDS), 2 * T0)
    second = (first + _np.repeat(_np.arange(2 * T0), FIELDS)) % FIELDS
    w0a = w0[:, first, second].reshape(H, T0, P).transpose(2, 1, 0)
    w0b = w0[:, second, first].reshape(H, T0, P).transpose(2, 1, 0)[:, :T0 - 1]

    consts = _np.zeros((P, GPQ + P + 2), _np.float32)
    consts[_np.arange(P), _np.arange(P) // DIM] = 1.0
    consts[_np.arange(P), GPQ + _np.arange(P)] = 1.0
    starts = [sum(sizes[:f]) for f in range(FIELDS)]
    consts[:, GPQ + P] = _np.tile([n - 1 for n in sizes], 2)
    consts[:, GPQ + P + 1] = _np.tile(starts, 2)

    def column(a):
        return _np.asarray(a).reshape(-1, P).T

    laid = {
        "ids": ids.transpose(1, 3, 0, 2).reshape(P, NCHUNK * GATHERS),
        "table": _np.concatenate(tables, axis=0),
        "dense_t": _np.asarray(inputs["dense_ctx"]).T,
        "consts": consts,
        "params": _np.concatenate([column(inputs[n]) for n in (
            "L0_rec_b0", "L0_rec_b1", "L0_rec_b2", "b_top1", "b_top2", "W_top3")], axis=1),
        "w0a": w0a, "w0b": w0b,
        "w1": w1.transpose(1, 3, 4, 2, 5, 0).reshape(P, FIELDS * H // P, H),
        "w2": w2.transpose(1, 2, 0), "wt1": inputs["W_top1"], "wt2": inputs["W_top2"],
    }
    nc = _bacc.Bacc("TRN2", target_bir_lowering=False, num_devices=1)
    arrays, args = {}, []
    for name, a in laid.items():
        a = _np.ascontiguousarray(a)
        arrays[f"in_{name}"] = a
        args.append(nc.dram_tensor(f"in_{name}", a.shape, _mybir.dt.from_np(a.dtype), kind="ExternalInput").ap())
    args.append(nc.dram_tensor("out_y", (BATCH, 1), _mybir.dt.float32, kind="ExternalOutput").ap())
    cin_tower(nc, *args)
    r = _run(nc, [arrays], core_ids=[0])
    return r.results[0]["out_y"]
```

```python
import concourse.bass as bass
from concourse import mybir
from contextlib import ExitStack

F32 = mybir.dt.float32
F32R = mybir.dt.float32r
I32 = mybir.dt.int32
ALU = mybir.AluOpType
ACT = mybir.ActivationFunctionType
AX_X = mybir.AxisListType.X

P = 128
BATCH, FIELDS, DIM, DENSE = 512, 64, 16, 16
H = 128
TOP1, TOP2 = 512, 256
CB = 32
NC = CB * DIM
NCHUNK = BATCH // CB
GC = 4
NG = NCHUNK // GC
GB = GC * CB
SHIFTS = FIELDS // 2 + 1
T0 = (SHIFTS + 1) // 2
QT = 2
ITEMS = 1 + (T0 - 1) // QT
ZRING = 3
GPQ = P // DIM
NQ = NC // P
UF = NC // H
BATCHES = NQ * FIELDS // UF // 4
UNITS = 4 * BATCHES
PERQ = BATCHES // NQ
STEPS = {"fold0": (0, 0), "fold1": (1, 1), "fold2": (2, 2), "add1": (3, 2), "fold3": (4, 3),
         "add2": (5, 4), "fold4": (6, 5), "add3": (7, 6)}
FOLDS = 5
LAST_BLOCK = len(STEPS) * NQ * NCHUNK - FOLDS
W2P = 16
W2F = FIELDS // W2P
W2RING = 4
W1P = 8
GATHERS = CB // 2

ITEM_AFTER = {1: 0, 6: 1, 11: 2, 17: 3, 23: 4, 30: 5, 36: 6, 43: 7, 50: 8}
G_AFTER = {20: 0, 25: 1, 30: 2, 34: 3}
X0T_AFTER = 29
W2_AFTER = [40 + 3 * p // 2 for p in range(W2P)]
MAKE_ITEM_AFTER = {1: 3, 2: 4, 4: 5, 5: 6, 7: 7, 9: 8, 11: 0, 12: 1, 14: 2}
MAKE_BD_AFTER = {3: (0, 1), 5: (2,), 6: (3,)}
COPY_G_AFTER = {5: 0, 6: 1, 7: 2, 9: 3}
COPY_X0T_AFTER = 7
X1_AFTER = 12
SPLIT_X1_AFTER = 13
X3_AFTER = 15


def item_tiles(r):
    return [T0 - 1] if r == 0 else list(range(QT * (r - 1), QT * r))


def at(g, c, per_chunk, more):
    return GC * per_chunk * g + (per_chunk * c + more)


def steps_before(g, c, q, name, done=False):
    place = STEPS[name][0] + (1 if done else 0)
    if isinstance(g, int) and GC * g + c == 0 and q == 0:
        return {"add1": 0, "add2": 1, "add3": 2}[name] + (1 if done else 0)
    return at(g, c, NQ * len(STEPS), len(STEPS) * q + place - FOLDS)


def cin_tower(nc, ids, table, dense_t, consts, params, b1_row, w0a, w0b, w1, w2, wt1, wt2, out):
    ctx = ExitStack()
    with ctx:
        def sb(name, shape, dt=F32):
            return ctx.enter_context(nc.sbuf_tensor(name, shape, dt))

        def pb(name, shape):
            return ctx.enter_context(nc.psum_tensor(name, shape, F32))

        def sem(name):
            return ctx.enter_context(nc.semaphore(name))

        x0_dram = nc.dram_tensor("x0_scratch", (GC, 2 * FIELDS, NC), F32, kind="Internal").ap()

        const_sb = sb("const_sb", [P, GPQ + P + 2])
        mask = const_sb[:, 0:GPQ]
        ident = const_sb[:, GPQ:GPQ + P]
        vmax = const_sb[:, GPQ + P:GPQ + P + 1]
        voff = const_sb[:, GPQ + P + 1:GPQ + P + 2]
        rows_sb = sb("rows_sb", [P, NCHUNK * GATHERS], I32)
        rows_chunk = sb("rows_chunk", [P, GC, GATHERS], I32)
        carrier = sb("carrier", [P, 1])
        xg = sb("xg", [P, GC, GATHERS * DIM])
        w0_sb = sb("w0_sb", [P, T0, H])
        w1h = sb("w1h", [P, FIELDS, H], F32R)
        w1l = sb("w1l", [P, FIELDS, H], F32R)
        w2_sb = sb("w2_sb", [P, W2RING, W2F, H])
        xi = sb("xi", [P, 2, NC])
        xs = sb("xs", [P, ZRING, QT, NC])
        z = sb("z", [P, ZRING, QT, NC])
        x1_sb = sb("x1_sb", [P, NC])
        x1h = sb("x1h", [P, 2, NC], F32R)
        x1l = sb("x1l", [P, 2, NC], F32R)
        x0t_sb = sb("x0t_sb", [P, 2, 2, P])
        batch_sb = sb("batch_sb", [P, PERQ, 3, NC])
        acc = sb("acc", [P, 3, NC])
        part = sb("part", [P, NC])
        x2t = sb("x2t", [P, 2, NQ, H])
        b1_sb = sb("b1_sb", [P, H])
        x0bd = sb("x0bd", [P, 2, GPQ, FIELDS])
        g_sb = sb("g_sb", [P, FIELDS, GB])
        sums = sb("sums", [P, 3, BATCH])
        M1, M2 = TOP1 // P, TOP2 // P
        params_sb = sb("params_sb", [P, 3 + M1 + 2 * M2])
        bias = params_sb[:, 0:3]
        bt_sb = params_sb[:, 3:3 + M1 + M2]
        wt3_sb = params_sb[:, 3 + M1 + M2:3 + M1 + 2 * M2]
        b2_sum = sb("b2_sum", [P, 1])
        ids_sb = x1_sb[:, 0:NCHUNK * GATHERS].bitcast(I32)
        w1_raw = g_sb
        w0b_sb = batch_sb[:].rearrange("p a b n -> p (a b n)")[:, 0:(T0 - 1) * H]\
            .rearrange("p (t o) -> p t o", o=H)
        flat = xs[:].rearrange("p a b n -> p (a b n)")
        wt1_sb = flat[:, 0:3 * TOP1].rearrange("p (k m) -> p k m", m=TOP1)
        wt2_sb = flat[:, 3 * TOP1:3 * TOP1 + M1 * TOP2].rearrange("p (k m) -> p k m", m=TOP2)
        dense_sb = flat[0:DENSE, 3 * TOP1 + M1 * TOP2:3 * TOP1 + M1 * TOP2 + BATCH]
        wt1d_sb = xi[0:DENSE, 0, :]
        zflat = z[:].rearrange("p a b n -> p (a b) n")
        h1_sb = zflat[:, 0:M1, :]
        h2_sb = zflat[:, M1:M1 + M2, :]
        y_sb = x1_sb[0:1, :]

        acc0 = pb("acc0", [P, NC])
        y_act_ps = [pb(f"y_act_ps_{i}", [P, NC]) for i in range(3)]
        y_dve_ps = [pb(f"y_dve_ps_{i}", [P, NC]) for i in range(2)]
        small_ps = pb("small_ps", [P, 512])
        x0t_ps = small_ps[:, 0:2 * P]
        s2_ps = small_ps[:, 2 * P:2 * P + CB]
        g_ps = pb("g_ps", [P, GPQ * FIELDS])
        g_last_ps = [g_ps, acc0]
        h1_ps = y_act_ps + y_dve_ps[0:1]
        h2_ps = [y_dve_ps[1], acc0]
        y_ps = g_ps[0:1, :]
        x3_ps = small_ps[:, 3 * P:3 * P + GB]

        const_loaded = sem("const_loaded")
        ids_loaded = sem("ids_loaded")
        params_loaded = sem("params_loaded")
        b1_loaded = sem("b1_loaded")
        rows_ready = sem("rows_ready")
        rows_copied = sem("rows_copied")
        gathered = [sem(f"gathered_{i}") for i in range(GC)]
        x0_stored = [sem(f"x0_stored_{i}") for i in range(GC)]
        w0_loaded = sem("w0_loaded")
        w0b_loaded = sem("w0b_loaded")
        w0_ready = sem("w0_ready")
        w1_loaded = [sem(f"w1_loaded_{i}") for i in range(2)]
        w1h_ready = sem("w1h_ready")
        w1l_ready = sem("w1l_ready")
        w2_loaded = [sem(f"w2_loaded_{i}") for i in range(W2RING)]
        b2_ready = sem("b2_ready")
        xi_loaded = [sem(f"xi_loaded_{i}") for i in range(2)]
        xs_loaded = [sem(f"xs_loaded_{i}") for i in range(ZRING)]
        z_ready = sem("z_ready")
        z_used = sem("z_used")
        x1_ready = sem("x1_ready")
        x1_split = sem("x1_split")
        x1_summed = sem("x1_summed")
        x0t_done = sem("x0t_done")
        x0t_ready = sem("x0t_ready")
        y_done = sem("y_done")
        y_act = sem("y_act")
        y_dve = sem("y_dve")
        x2_step = sem("x2_step")
        x0bd_ready = sem("x0bd_ready")
        s2_done = sem("s2_done")
        s2_ready = sem("s2_ready")
        g_done = sem("g_done")
        g_ready = sem("g_ready")
        w2_used = sem("w2_used")
        x3_ready = sem("x3_ready")
        top_loaded = sem("top_loaded")
        h_done = sem("h_done")
        h_ready = sem("h_ready")
        y_stored = sem("y_stored")

        block = ctx.enter_context(nc.Block())

        def run_chunks(eng, chunk):
            chunk(0, 0, 0)
            with eng.Fori(0, NG - 1) as g:
                for c in range(1, GC + 1):
                    chunk(g, c, None)
            for c in range(1, GC):
                chunk(NG - 1, c, GC * (NG - 1) + c)

        def scale_of(par, q, f):
            col = (q // 2) * FIELDS + f
            return x0t_sb[:, par, q % 2, col:col + 1]

        @block.sync
        def _(sp):
            sp.dma_start(ids_sb, ids).then_inc(ids_loaded, 16)
            sp.dma_start(const_sb[:], consts).then_inc(const_loaded, 16)
            for half in range(2):
                h = FIELDS // 2
                sp.dma_start(w1_raw[:, half * h:(half + 1) * h, :], w1[:, half * h:(half + 1) * h, :])\
                    .then_inc(w1_loaded[half], 16)
            sp.dma_start(b1_sb[:], b1_row.to_broadcast([P, H])).then_inc(b1_loaded, 16)

            def store_x0(uses, s):
                sp.wait_ge(gathered[s], 16 * GATHERS * uses)
                for half in range(2):
                    for copy in range(2):
                        sp.dma_start(x0_dram[s, copy * FIELDS:(copy + 1) * FIELDS, half * NC // 2:(half + 1) * NC // 2],
                                     xg[half * FIELDS:(half + 1) * FIELDS, s, :]).then_inc(x0_stored[s], 16)

            def load_xi(s, par):
                for s2 in range(2):
                    sp.dma_start(xi[s2 * FIELDS:(s2 + 1) * FIELDS, par, :],
                                 x0_dram[s, 0:FIELDS, :]).then_inc(xi_loaded[par], 16)

            def load_xs(s, r):
                tiles = item_tiles(r)
                for s2 in range(1 if r == 0 else 2):
                    first = s2 + 2 * tiles[0]
                    src = x0_dram[s, first:first + FIELDS, :]
                    src = bass.AP(src.tensor, src.offset, [[NC, FIELDS], [2 * NC, len(tiles)], [1, NC]])
                    sp.dma_start(xs[s2 * FIELDS:(s2 + 1) * FIELDS, r % ZRING, 0:len(tiles), :], src)\
                        .then_inc(xs_loaded[r % ZRING], 16 if r else 32)

            def load_chunk(g, c, items, first=False):
                s = c % GC
                if items[0] == 0:
                    sp.wait_ge(x0_stored[s], 64 * g + 64 * (c // GC + 1))
                    load_xi(s, c % 2)
                for r in items:
                    if not (first and r < ZRING):
                        sp.wait_ge(z_ready, at(g, c, ITEMS, r - ZRING + 1))
                    load_xs(s, r)

            store_x0(1, 0)
            load_chunk(0, 0, range(ITEMS), True)
            store_x0(1, 1)
            load_chunk(0, 1, range(ZRING))

            def chunk(g, c, k):
                if k != NCHUNK - 1:
                    load_chunk(g, c + 1, range(ZRING, ITEMS))
                if not (k is not None and k + 2 >= NCHUNK):
                    store_x0(g + (c + 2) // GC + 1, (c + 2) % GC)
                    load_chunk(g, c + 2, range(ZRING))

            run_chunks(sp, chunk)

            sp.wait_ge(z_ready, ITEMS * NCHUNK)
            sp.dma_start(wt1_sb, wt1[0:3 * H, :].rearrange("(k p) m -> p k m", p=H)).then_inc(top_loaded, 16)
            sp.dma_start(wt1d_sb, wt1[3 * H:3 * H + DENSE, :]).then_inc(top_loaded, 16)
            sp.dma_start(wt2_sb, wt2.rearrange("(k p) m -> p k m", p=P)).then_inc(top_loaded, 16)
            sp.dma_start(dense_sb, dense_t).then_inc(top_loaded, 16)
            sp.wait_ge(h_ready, M1 + M2 + 1)
            sp.dma_start(out.rearrange("b a -> a b"), y_sb).then_inc(y_stored, 16)
            sp.wait_ge(y_stored, 16)

        @block.gpsimd
        def _(pool):
            pool.wait_ge(rows_ready, 1)

            def gather(chunk, copies, s):
                nc.gpsimd.tensor_copy(rows_chunk[:, s, :], rows_sb[:, bass.ds(GATHERS * chunk, GATHERS)])\
                    .then_inc(rows_copied, 1)
                pool.wait_ge(rows_copied, copies)
                nc.gpsimd.tensor_tensor(carrier[:], vmax, voff, ALU.add)
                for j in range(GATHERS):
                    nc.gpsimd.indirect_dma_start(
                        out=xg[:, s, j * DIM:(j + 1) * DIM], out_offset=None, in_=table,
                        in_offset=bass.IndirectOffsetOnAxis(ap=rows_chunk[:, s, j:j + 1], axis=0))\
                        .then_inc(gathered[s], 16)

            for c in range(GC):
                gather(c, c + 1, c)

            with pool.Fori(0, NG - 1) as g:
                for c in range(GC):
                    pool.wait_ge(x0t_done, GC * g + c + 1)
                    pool.wait_ge(x0_stored[c], 64 * g + 64)
                    gather(GC * g + c + GC, GC * g + c + GC + 1, c)

        @block.scalar
        def _(act):
            act.dma_start(w0_sb[:], w0a).then_inc(w0_loaded, 16)
            act.dma_start(w0b_sb, w0b).then_inc(w0b_loaded, 16)
            act.dma_start(params_sb[:], params).then_inc(params_loaded, 16)

            def load_w2(p):
                act.dma_start(w2_sb[:, p % W2RING, :, :], w2[:, p * W2F:(p + 1) * W2F, :])\
                    .then_inc(w2_loaded[p % W2RING], 16)

            act.wait_ge(params_loaded, 16)
            nc.scalar.mul(b2_sum[:], bias[:, 2:3], float(DIM)).then_inc(b2_ready, 1)
            for p in range(W1P):
                fs = slice(p * FIELDS // W1P, (p + 1) * FIELDS // W1P)
                act.wait_ge(w1_loaded[2 * p // W1P], 16)
                nc.scalar.activation(w1h[:, fs, :], w1_raw[:, fs, :], ACT.Copy).then_inc(w1h_ready, 1)

            def copy_x0t(par, done):
                act.wait_ge(x0t_done, done)
                nc.scalar.activation(x0t_sb[:, par, :, :].rearrange("p m c -> p (m c)"), x0t_ps, ACT.Copy)\
                    .then_inc(x0t_ready, 1)

            def make_x1(g, c, m):
                act.wait_ge(z_used, at(g, c, ITEMS, 2 * ITEMS))
                if m != 0:
                    act.wait_ge(x1_split, at(g, c, 1, 1))
                    act.wait_ge(x1_summed, at(g, c, 1, 1))
                par = (c + 1) % 2
                nc.scalar.activation(x1h[:, par, :], acc0[:], ACT.Identity, bias=bias[:, 0:1])
                nc.scalar.activation(x1_sb[:], acc0[:], ACT.Identity, bias=bias[:, 0:1]).then_inc(x1_ready, 1)

            copy_x0t(0, 1)
            make_x1(0, -1, 0)

            def copy_g(g, c, q):
                act.wait_ge(g_done, at(g, c, NQ, q + 1 - NQ))
                bank = g_last_ps[q % 2] if isinstance(g, int) and GC * g + c == NCHUNK else g_ps
                b = (c - 1) % GC * CB + q * GPQ
                nc.scalar.activation(g_sb[:, :, b:b + GPQ].rearrange("p f b -> p b f"),
                                     bank[:].rearrange("p (b f) -> p b f", f=FIELDS),
                                     ACT.Copy).then_inc(g_ready, 1)

            def copy_s2(g, c):
                act.wait_ge(s2_done, at(g, c, 1, 0))
                nc.scalar.activation(sums[:, 1, bass.ds(at(g, c, CB, -CB), CB)], s2_ps, ACT.Copy)\
                    .then_inc(s2_ready, 1)

            def copy_x3(g):
                act.wait_ge(w2_used, W2P * g + W2P)
                nc.scalar.activation(sums[:, 2, bass.ds(GB * g, GB)], x3_ps, ACT.Identity,
                                     bias=b2_sum[:]).then_inc(x3_ready, 1)

            def chunk(g, c, k):
                par = c % 2
                act.wait_ge(x0t_ready, at(g, c, 1, 1))
                for j in range(BATCHES):
                    q, b = j // PERQ, j % PERQ
                    if q > 0:
                        act.wait_ge(x2_step, steps_before(g, c, q - 1, f"add{max(b, 1)}", done=True))
                    elif k != 0:
                        act.wait_ge(x2_step, steps_before(g, c - 1, NQ - 1, f"add{max(b, 1)}", done=True))
                    for i in range(3):
                        act.wait_ge(y_done, at(g, c, UNITS, 4 * j + i + 1))
                        for n in range(UF):
                            f = UF * (4 * b + i) + n
                            last = nc.scalar.activation(batch_sb[:, b, i, n * H:(n + 1) * H],
                                                        y_act_ps[i][:, n * H:(n + 1) * H], ACT.Copy,
                                                        scale=scale_of(par, q, f))
                        last.then_inc(y_act, 1)
                        for p in range(W2P - W2RING):
                            if c == GC and (W2_AFTER[p] + 1, W2_AFTER[p] + 2)[W2_AFTER[p] % 4 == 2] == 4 * j + i:
                                act.wait_ge(w2_used, W2P * g + p + 1)
                                load_w2(p + W2RING)
                    if k != 0 and j in COPY_G_AFTER:
                        if COPY_G_AFTER[j] == 0:
                            copy_s2(g, c)
                        copy_g(g, c, COPY_G_AFTER[j])
                    if k != NCHUNK - 1 and j == COPY_X0T_AFTER:
                        if k != 0:
                            act.wait_ge(x0bd_ready, at(g, c, NQ, 0))
                        copy_x0t(1 - par, at(g, c, 1, 2))
                    if k != NCHUNK - 1 and j == X1_AFTER:
                        make_x1(g, c, 1)
                    if (c == GC or k == NCHUNK - 1) and j == 0:
                        for p in range(W2RING):
                            load_w2(p)
                    if c == GC and j == X3_AFTER:
                        copy_x3(g)

            run_chunks(act, chunk)

            copy_s2(NG - 1, GC)
            for q in range(NQ):
                copy_g(NG - 1, GC, q)
            for p in range(W2RING, W2P):
                act.wait_ge(w2_used, W2P * (NG - 1) + p - W2RING + 1)
                load_w2(p)
            copy_x3(NG - 1)

            for m in range(M1):
                act.wait_ge(h_done, m + 1)
                nc.scalar.activation(h1_sb[:, m, :], h1_ps[m][:], ACT.Relu, bias=bt_sb[:, m:m + 1])\
                    .then_inc(h_ready, 1)
            for m in range(M2):
                act.wait_ge(h_done, M1 + m + 1)
                nc.scalar.activation(h2_sb[:, m, :], h2_ps[m][:], ACT.Relu, bias=bt_sb[:, M1 + m:M1 + m + 1])\
                    .then_inc(h_ready, 1)
            act.wait_ge(h_done, M1 + M2 + 1)
            nc.scalar.activation(y_sb, y_ps, ACT.Copy).then_inc(h_ready, 1)

        @block.vector
        def _(dve):
            dve.wait_ge(ids_loaded, 16)
            dve.wait_ge(const_loaded, 16)
            nc.vector.tensor_scalar(rows_sb[:], ids_sb, vmax, voff, ALU.min, ALU.add).then_inc(rows_ready, 1)
            dve.wait_ge(w0_loaded, 16)
            dve.wait_ge(w0b_loaded, 16)
            nc.vector.tensor_tensor(w0_sb[FIELDS:P, 0, :], w0_sb[FIELDS:P, 0, :], w0b_sb[FIELDS:P, 0, :], ALU.add)
            nc.vector.tensor_tensor(w0_sb[:, 1:T0 - 1, :], w0_sb[:, 1:T0 - 1, :], w0b_sb[:, 1:T0 - 1, :], ALU.add)\
                .then_inc(w0_ready, 1)
            for p in range(W1P):
                fs = slice(p * FIELDS // W1P, (p + 1) * FIELDS // W1P)
                dve.wait_ge(w1h_ready, p + 1)
                nc.vector.tensor_tensor(w1l[:, fs, :], w1_raw[:, fs, :], w1h[:, fs, :].bitcast(F32), ALU.subtract)\
                    .then_inc(w1l_ready, 1)

            def make_item(g, c, r, first):
                par = (c + 1) % 2
                if r == 0:
                    dve.wait_ge(xi_loaded[par], 32 * (GC // 2) * g + 32 * ((c + 1) // 2 + 1))
                per = ITEMS // ZRING
                dve.wait_ge(xs_loaded[r % ZRING], at(g, c, 32 * per, 32 * (per + r // ZRING + 1)))
                if not (first and r < ZRING):
                    dve.wait_ge(z_used, at(g, c, ITEMS, ITEMS + r - ZRING + 1))
                tiles = len(item_tiles(r))
                rows = FIELDS if r == 0 else P
                nc.vector.tensor_tensor(z[0:rows, r % ZRING, 0:tiles, :],
                                        xi[0:rows, par, :].unsqueeze(1).to_broadcast([rows, tiles, NC]),
                                        xs[0:rows, r % ZRING, 0:tiles, :], ALU.mult).then_inc(z_ready, 1)

            def split_x1(g, c):
                par = (c + 1) % 2
                dve.wait_ge(x1_ready, at(g, c, 1, 2))
                nc.vector.tensor_tensor(x1l[:, par, :], x1_sb[:], x1h[:, par, :].bitcast(F32), ALU.subtract)\
                    .then_inc(x1_split, 1)
                nc.vector.tensor_reduce(sums[:, 0, bass.ds(at(g, c, CB, CB), CB)],
                                        x1_sb[:].rearrange("p (b d) -> p b d", d=DIM),
                                        AX_X, ALU.add).then_inc(x1_summed, 1)

            for r in range(ITEMS):
                make_item(0, -1, r, True)
            split_x1(0, -1)
            for r in range(ZRING):
                make_item(0, 0, r, False)
            dve.wait_ge(b1_loaded, 16)

            def step(g, c, q, name, out, in0, in1):
                place, needs = STEPS[name]
                first = isinstance(g, int) and GC * g + c == 0 and q == 0
                needed = steps_before(g, c, q, name) - (0 if first else place - needs)
                if not (first and name == "add1"):
                    dve.wait_ge(x2_step, needed)
                nc.vector.tensor_tensor(out, in0, in1, ALU.add).then_inc(x2_step, 1)

            def fold(g, c, q, n):
                if n == 0:
                    step(g, c, q, "fold0", part[:], acc[:, 0, :], acc[:, 1, :])
                elif n == 1:
                    step(g, c, q, "fold1", part[:], part[:], acc[:, 2, :])
                elif n == 2:
                    step(g, c, q, "fold2", part[:, 0:2 * H], part[:, 0:2 * H], part[:, 2 * H:4 * H])
                elif n == 3:
                    step(g, c, q, "fold3", part[:, 0:H], part[:, 0:H], part[:, H:2 * H])
                else:
                    par = c % 2 if q > 0 else (c - 1) % 2
                    step(g, c, q, "fold4", x2t[:, par, (q - 1) % NQ, :], part[:, 0:H], b1_sb[:])

            def make_bd(g, c, q):
                par = (c - 1) % 2
                if q >= 2 or isinstance(g, int) and GC * g + c == NCHUNK:
                    dve.wait_ge(g_done, at(g, c, NQ, q - 1 - NQ))
                col = q // 2 * FIELDS
                nc.vector.tensor_tensor(
                    x0bd[:, q % 2, :, :],
                    x0t_sb[:, par, q % 2, col:col + FIELDS].unsqueeze(1).to_broadcast([P, GPQ, FIELDS]),
                    mask.unsqueeze(2).to_broadcast([P, GPQ, FIELDS]), ALU.mult).then_inc(x0bd_ready, 1)

            def chunk(g, c, k):
                par = c % 2
                dve.wait_ge(x0t_ready, at(g, c, 1, 1))
                for j in range(BATCHES):
                    q, b = j // PERQ, j % PERQ
                    dve.wait_ge(y_act, at(g, c, 3 * BATCHES, 3 * j + 1))
                    dve.wait_ge(y_done, at(g, c, UNITS, 4 * j + 4))
                    for n in range(UF):
                        f = UF * (4 * b + 3) + n
                        slot = batch_sb[:, b, 0, n * H:(n + 1) * H]
                        last = nc.vector.scalar_tensor_tensor(
                            out=slot, in0=y_dve_ps[j % 2][:, n * H:(n + 1) * H], scalar=scale_of(par, q, f),
                            in1=slot, op0=ALU.mult, op1=ALU.add)
                    last.then_inc(y_dve, 1)
                    folds = k != 0 or q > 0
                    if folds:
                        fold(g, c, q, 0 if b == 0 else b + 1)
                    if j in MAKE_ITEM_AFTER:
                        r = MAKE_ITEM_AFTER[j]
                        ahead = 1 if r < ZRING else 0
                        if not (k is not None and k + 1 + ahead >= NCHUNK):
                            make_item(g, c + ahead, r, False)
                    if b == 0 and folds:
                        fold(g, c, q, 1)
                    if b > 0:
                        dve.wait_ge(y_act, at(g, c, 3 * BATCHES, 3 * j + 3))
                        dve.wait_ge(y_dve, at(g, c, BATCHES, j + 1))
                        step(g, c, q, f"add{b}", acc[:], batch_sb[:, 0, :, :] if b == 1 else acc[:], batch_sb[:, b, :, :])
                    if k != 0:
                        for e in MAKE_BD_AFTER.get(j, ()):
                            make_bd(g, c, e)
                    if k == NCHUNK - 1 and j >= BATCHES - 4 and j < BATCHES - 2:
                        make_bd(g, c + 1, j - (BATCHES - 4))
                    if k != NCHUNK - 1 and j == SPLIT_X1_AFTER:
                        split_x1(g, c)

            run_chunks(dve, chunk)
            for n in range(FOLDS):
                dve.wait_ge(x2_step, LAST_BLOCK + n)
                out, in0, in1 = ((part[:], acc[:, 0, :], acc[:, 1, :]), (part[:], part[:], acc[:, 2, :]),
                                 (part[:, 0:2 * H], part[:, 0:2 * H], part[:, 2 * H:4 * H]),
                                 (part[:, 0:H], part[:, 0:H], part[:, H:2 * H]),
                                 (x2t[:, (NCHUNK - 1) % 2, NQ - 1, :], part[:, 0:H], b1_sb[:]))[n]
                nc.vector.tensor_tensor(out, in0, in1, ALU.add).then_inc(x2_step, 1)
            for q in range(2, NQ):
                make_bd(NG - 1, GC, q)

        @block.tensor
        def _(pe):
            pe.wait_ge(w0_ready, 1)

            def use_item(g, c, r):
                pe.wait_ge(z_ready, at(g, c, ITEMS, ITEMS + r + 1))
                tiles = item_tiles(r)
                rows = FIELDS if r == 0 else P
                for n, t in enumerate(tiles):
                    mm = nc.tensor.matmul(acc0[:], w0_sb[0:rows, t, :], z[0:rows, r % ZRING, n, :],
                                          start=(r == 0), stop=(r == ITEMS - 1 and n == len(tiles) - 1))
                mm.then_inc(z_used, 1)

            def transpose_x0(s, uses):
                pe.wait_ge(gathered[s], 16 * GATHERS * uses)
                for m in range(2):
                    mm = nc.tensor.transpose(x0t_ps[:, m * P:(m + 1) * P], xg[:, s, m * P:(m + 1) * P], ident)
                mm.then_inc(x0t_done, 1)

            pe.wait_ge(const_loaded, 16)
            transpose_x0(0, 1)
            for r in range(ITEMS):
                use_item(0, -1, r)
            pe.wait_ge(w1l_ready, W1P)
            pe.wait_ge(w1h_ready, W1P)

            def make_g(g, c, q):
                par = (c - 1) % 2
                last = isinstance(g, int) and GC * g + c == NCHUNK
                bank = g_last_ps[q % 2] if last else g_ps
                if q == 0:
                    pe.wait_ge(x2_step, LAST_BLOCK + FOLDS if last else steps_before(g, c, 0, "fold4", done=True))
                    for e in range(NQ):
                        mm = nc.tensor.matmul(s2_ps[:, e * GPQ:(e + 1) * GPQ], x2t[:, par, e, :], mask,
                                              start=True, stop=True)
                    mm.then_inc(s2_done, 1)
                elif not (last and q == 1):
                    pe.wait_ge(g_ready, at(g, c, NQ, q - NQ - (1 if last else 0)))
                pe.wait_ge(x0bd_ready, at(g, c, NQ, q + 1 - NQ))
                nc.tensor.matmul(bank[:], x2t[:, par, q, :], x0bd[:, q % 2, :, :].rearrange("p b f -> p (b f)"),
                                 start=True, stop=True).then_inc(g_done, 1)

            def use_w2(g, p):
                if p == 0:
                    pe.wait_ge(g_ready, NQ * GC * g + NQ * GC)
                pe.wait_ge(w2_loaded[p % W2RING], 16 * (W2P // W2RING) * g + 16 * (p // W2RING + 1))
                for n in range(W2F):
                    f = p * W2F + n
                    mm = nc.tensor.matmul(x3_ps, w2_sb[:, p % W2RING, n, :], g_sb[:, f, :],
                                          start=(f == 0), stop=(f == FIELDS - 1))
                mm.then_inc(w2_used, 1)

            def chunk(g, c, k):
                par = c % 2
                pe.wait_ge(x1_split, at(g, c, 1, 1))
                for u in range(UNITS):
                    q, j, bank = u // (4 * PERQ), u // 4, u % 4
                    fs = slice(UF * (u % (4 * PERQ)), UF * (u % (4 * PERQ)) + UF)
                    if bank < 3:
                        y_ps = y_act_ps[bank]
                        if not (k == 0 and j == 0):
                            pe.wait_ge(y_act, at(g, c, 3 * BATCHES, 3 * (j - 1) + bank + 1))
                    else:
                        y_ps = y_dve_ps[j % 2]
                        if not (k == 0 and j < 2):
                            pe.wait_ge(y_dve, at(g, c, BATCHES, j - 1))
                    cols = slice(q * P, (q + 1) * P)
                    nc.tensor.matmul(y_ps[:], x1h[:, par, cols], w1h[:, fs, :].rearrange("h f o -> h (f o)"),
                                     start=True, stop=False)
                    nc.tensor.matmul(y_ps[:], x1h[:, par, cols], w1l[:, fs, :].rearrange("h f o -> h (f o)"),
                                     start=False, stop=False)
                    nc.tensor.matmul(y_ps[:], x1l[:, par, cols], w1h[:, fs, :].rearrange("h f o -> h (f o)"),
                                     start=False, stop=True).then_inc(y_done, 1)
                    if k != NCHUNK - 1 and u in ITEM_AFTER:
                        use_item(g, c, ITEM_AFTER[u])
                    if k != 0 and u in G_AFTER:
                        make_g(g, c, G_AFTER[u])
                    if k != NCHUNK - 1 and u == X0T_AFTER:
                        transpose_x0((c + 1) % GC, g + (c + 1) // GC + 1)
                    if c == GC and u in W2_AFTER:
                        use_w2(g, W2_AFTER.index(u))

            run_chunks(pe, chunk)

            def top1(m, n):
                mm = nc.tensor.matmul(h1_ps[m][:], wt1_sb[:, n, m * P:(m + 1) * P], sums[:, n, :],
                                      start=False, stop=(n == 2))
                if n == 2:
                    mm.then_inc(h_done, 1)

            pe.wait_ge(top_loaded, 64)
            pe.wait_ge(x1_summed, NCHUNK)
            for m in range(M1):
                if m < M1 - 1:
                    pe.wait_ge(y_act, 3 * BATCHES * NCHUNK - 2 + m)
                else:
                    pe.wait_ge(y_dve, BATCHES * NCHUNK - 1)
                nc.tensor.matmul(h1_ps[m][:], wt1d_sb[:, m * P:(m + 1) * P], dense_sb, start=True, stop=False)
                top1(m, 0)
            for q in range(NQ):
                make_g(NG - 1, GC, q)
                if q > 0:
                    pe.wait_ge(s2_ready, NCHUNK)
                    top1(q - 1, 1)
            top1(M1 - 1, 1)
            for p in range(W2P):
                use_w2(NG - 1, p)
            pe.wait_ge(x3_ready, NG)
            for m in range(M1):
                top1(m, 2)
            pe.wait_ge(y_dve, BATCHES * NCHUNK)
            for n in range(M1):
                pe.wait_ge(h_ready, n + 1)
                for m in range(M2):
                    mm = nc.tensor.matmul(h2_ps[m][:], wt2_sb[:, n, m * P:(m + 1) * P], h1_sb[:, n, :],
                                          start=(n == 0), stop=(n == M1 - 1))
                    if n == M1 - 1:
                        mm.then_inc(h_done, 1)
            for m in range(M2):
                pe.wait_ge(h_ready, M1 + m + 1)
                mm = nc.tensor.matmul(y_ps, wt3_sb[:, m:m + 1], h2_sb[:, m, :], start=(m == 0), stop=(m == M2 - 1))
            mm.then_inc(h_done, 1)


def kernel(**inputs):
    import numpy as _np
    import concourse.bacc as _bacc
    from concourse import mybir as _mybir
    from concourse.bass_utils import run_bass_kernel_spmd as _run

    tables = [_np.asarray(inputs[f"tbl_{f}"]) for f in range(FIELDS)]
    sizes = [t.shape[0] for t in tables]
    ids = _np.asarray(inputs["ids"]).reshape(NCHUNK, 2, GATHERS, FIELDS)
    w0 = _np.asarray(inputs["L0_rec_W0"]).reshape(H, FIELDS, FIELDS)
    w1 = _np.asarray(inputs["L0_rec_W1"]).reshape(H, H, FIELDS)
    w2 = _np.asarray(inputs["L0_rec_W2"]).reshape(H, H, FIELDS)

    first = _np.tile(_np.arange(FIELDS), 2 * T0)
    second = (first + _np.repeat(_np.arange(2 * T0), FIELDS)) % FIELDS
    w0a = w0[:, first, second].reshape(H, T0, P).transpose(2, 1, 0)
    w0b = w0[:, second, first].reshape(H, T0, P).transpose(2, 1, 0)[:, :T0 - 1]

    consts = _np.zeros((P, GPQ + P + 2), _np.float32)
    consts[_np.arange(P), _np.arange(P) // DIM] = 1.0
    consts[_np.arange(P), GPQ + _np.arange(P)] = 1.0
    starts = [sum(sizes[:f]) for f in range(FIELDS)]
    consts[:, GPQ + P] = _np.tile([n - 1 for n in sizes], 2)
    consts[:, GPQ + P + 1] = _np.tile(starts, 2)

    def column(a):
        return _np.asarray(a).reshape(-1, P).T

    laid = {
        "ids": ids.transpose(1, 3, 0, 2).reshape(P, NCHUNK * GATHERS),
        "table": _np.concatenate(tables, axis=0),
        "dense_t": _np.asarray(inputs["dense_ctx"]).T,
        "consts": consts,
        "params": _np.concatenate([column(inputs[n]) for n in (
            "L0_rec_b0", "L0_rec_b1", "L0_rec_b2", "b_top1", "b_top2", "W_top3")], axis=1),
        "b1_row": _np.asarray(inputs["L0_rec_b1"]).reshape(1, H),
        "w0a": w0a, "w0b": w0b,
        "w1": w1.transpose(1, 2, 0),
        "w2": w2.transpose(1, 2, 0), "wt1": inputs["W_top1"], "wt2": inputs["W_top2"],
    }
    nc = _bacc.Bacc("TRN2", target_bir_lowering=False, num_devices=1)
    arrays, args = {}, []
    for name, a in laid.items():
        a = _np.ascontiguousarray(a)
        arrays[f"in_{name}"] = a
        args.append(nc.dram_tensor(f"in_{name}", a.shape, _mybir.dt.from_np(a.dtype), kind="ExternalInput").ap())
    args.append(nc.dram_tensor("out_y", (BATCH, 1), _mybir.dt.float32, kind="ExternalOutput").ap())
    cin_tower(nc, *args)
    r = _run(nc, [arrays], core_ids=[0])
    return r.results[0]["out_y"]
```

```python
import concourse.bass as bass
from concourse import mybir
from contextlib import ExitStack

F32 = mybir.dt.float32
F32R = mybir.dt.float32r
I32 = mybir.dt.int32
ALU = mybir.AluOpType
ACT = mybir.ActivationFunctionType
AX_X = mybir.AxisListType.X

P = 128
BATCH, FIELDS, DIM, DENSE = 512, 64, 16, 16
H = 128
TOP1, TOP2 = 512, 256
CB = 32
NC = CB * DIM
NCHUNK = BATCH // CB
GC = 4
NG = NCHUNK // GC
GB = GC * CB
SHIFTS = FIELDS // 2 + 1
T0 = (SHIFTS + 1) // 2
QT = 2
ITEMS = 1 + (T0 - 1) // QT
ZRING = 3
GPQ = P // DIM
NQ = NC // P
UF = NC // H
BATCHES = NQ * FIELDS // UF // 4
UNITS = 4 * BATCHES
PERQ = BATCHES // NQ
STEPS = {"fold0": (0, 0), "fold1": (1, 1), "add1": (2, 1), "add2": (3, 3), "add3": (4, 4)}
FOLDS = 2
LAST_BLOCK = len(STEPS) * NQ * NCHUNK - FOLDS
W2P = 16
W2F = FIELDS // W2P
W2RING = 4
W1P = 8
GATHERS = CB // 2

ITEM_AFTER = {1: 0, 6: 1, 11: 2, 16: 3, 22: 4, 29: 5, 37: 6, 44: 7, 51: 8}
G_AFTER = {20: 0, 25: 1, 30: 2, 34: 3}
X0T_AFTER = 29
W2_AFTER = [40 + 3 * p // 2 for p in range(W2P)]
MAKE_ITEM_AFTER = {1: 3, 2: 4, 4: 5, 5: 6, 7: 7, 9: 8, 11: 0, 12: 1, 14: 2}
MAKE_BD_AFTER = {1: (0,), 3: (1,), 5: (2,), 6: (3,)}
COPY_G_AFTER = {5: 0, 6: 1, 7: 2, 8: 3}
COPY_X0T_AFTER = 7
X1_AFTER = 12
SPLIT_X1_AFTER = 13
X3_AFTER = 15


def item_tiles(r):
    return [T0 - 1] if r == 0 else list(range(QT * (r - 1), QT * r))


def at(g, c, per_chunk, more):
    return GC * per_chunk * g + (per_chunk * c + more)


def steps_before(g, c, q, name, done=False):
    place = STEPS[name][0] + (1 if done else 0)
    if isinstance(g, int) and GC * g + c == 0 and q == 0:
        return {"add1": 0, "add2": 1, "add3": 2}[name] + (1 if done else 0)
    return at(g, c, NQ * len(STEPS), len(STEPS) * q + place - FOLDS)


def cin_tower(nc, ids, table, dense_t, consts, params, b1_row, w0a, w0b, w1, w2, wt1, wt2, out):
    ctx = ExitStack()
    with ctx:
        def sb(name, shape, dt=F32):
            return ctx.enter_context(nc.sbuf_tensor(name, shape, dt))

        def pb(name, shape):
            return ctx.enter_context(nc.psum_tensor(name, shape, F32))

        def sem(name):
            return ctx.enter_context(nc.semaphore(name))

        x0_dram = nc.dram_tensor("x0_scratch", (GC, 2 * FIELDS, NC), F32, kind="Internal").ap()

        const_sb = sb("const_sb", [P, GPQ + P + 2])
        mask = const_sb[:, 0:GPQ]
        ident = const_sb[:, GPQ:GPQ + P]
        vmax = const_sb[:, GPQ + P:GPQ + P + 1]
        voff = const_sb[:, GPQ + P + 1:GPQ + P + 2]
        rows_sb = sb("rows_sb", [P, NCHUNK * GATHERS], I32)
        rows_chunk = sb("rows_chunk", [P, GC, GATHERS], I32)
        carrier = sb("carrier", [P, 1])
        xg = sb("xg", [P, GC, GATHERS * DIM])
        w0_sb = sb("w0_sb", [P, T0, H])
        w1h = sb("w1h", [P, FIELDS, H], F32R)
        w1l = sb("w1l", [P, FIELDS, H], F32R)
        w2_sb = sb("w2_sb", [P, W2RING, W2F, H])
        xi = sb("xi", [P, 2, NC])
        xs = sb("xs", [P, ZRING, QT, NC])
        z = sb("z", [P, ZRING, QT, NC])
        x1h = sb("x1h", [P, 2, NC], F32R)
        x1l = sb("x1l", [P, 2, NC], F32R)
        x0t_sb = sb("x0t_sb", [P, 2, 2, P])
        batch_sb = sb("batch_sb", [P, PERQ, 3, NC])
        acc = sb("acc", [P, 3, NC])
        part = sb("part", [P, H])
        x2t = sb("x2t", [P, 2, NQ, H])
        b1_sb = sb("b1_sb", [P, H])
        x0bd = sb("x0bd", [P, 2, GPQ, FIELDS])
        g_sb = sb("g_sb", [P, FIELDS, GB])
        sums = sb("sums", [P, 3, BATCH])
        M1, M2 = TOP1 // P, TOP2 // P
        params_sb = sb("params_sb", [P, 3 + M1 + 2 * M2])
        bias = params_sb[:, 0:3]
        bt_sb = params_sb[:, 3:3 + M1 + M2]
        wt3_sb = params_sb[:, 3 + M1 + M2:3 + M1 + 2 * M2]
        bias_sums = sb("bias_sums", [P, 3])
        ids_sb = acc[:, 0, 0:NCHUNK * GATHERS].bitcast(I32)
        w1_raw = g_sb
        w0b_sb = batch_sb[:].rearrange("p a b n -> p (a b n)")[:, 0:(T0 - 1) * H]\
            .rearrange("p (t o) -> p t o", o=H)
        flat = xs[:].rearrange("p a b n -> p (a b n)")
        wt1_sb = flat[:, 0:3 * TOP1].rearrange("p (k m) -> p k m", m=TOP1)
        wt2_sb = flat[:, 3 * TOP1:3 * TOP1 + M1 * TOP2].rearrange("p (k m) -> p k m", m=TOP2)
        dense_sb = flat[0:DENSE, 3 * TOP1 + M1 * TOP2:3 * TOP1 + M1 * TOP2 + BATCH]
        wt1d_sb = xi[0:DENSE, 0, :]
        zflat = z[:].rearrange("p a b n -> p (a b) n")
        h1_sb = zflat[:, 0:M1, :]
        h2_sb = zflat[:, M1:M1 + M2, :]
        y_sb = acc[0:1, 0, :]
        w2_rest = batch_sb[:].rearrange("p a b n -> p (a b n)")[:, 0:(W2P - W2RING) * W2F * H]\
            .rearrange("p (f o) -> p f o", o=H)

        acc0 = pb("acc0", [P, NC])
        y_act_ps = [pb(f"y_act_ps_{i}", [P, NC]) for i in range(3)]
        y_dve_ps = [pb(f"y_dve_ps_{i}", [P, NC]) for i in range(2)]
        small_ps = pb("small_ps", [P, 512])
        x0t_ps = small_ps[:, 0:2 * P]
        s2_ps = small_ps[:, 2 * P:2 * P + CB]
        g_ps = pb("g_ps", [P, GPQ * FIELDS])
        g_last_ps = [g_ps, acc0]
        h1_ps = y_act_ps + y_dve_ps[0:1]
        h2_ps = [y_dve_ps[1], acc0]
        y_ps = g_ps[0:1, :]
        x3_ps = small_ps[:, 3 * P:3 * P + GB]

        const_loaded = sem("const_loaded")
        ids_loaded = sem("ids_loaded")
        params_loaded = sem("params_loaded")
        b1_loaded = sem("b1_loaded")
        w2_rest_loaded = [sem(f"w2_rest_loaded_{i}") for i in range(W2P // W2RING - 1)]
        rows_ready = sem("rows_ready")
        rows_copied = sem("rows_copied")
        gathered = [sem(f"gathered_{i}") for i in range(GC)]
        x0_stored = [sem(f"x0_stored_{i}") for i in range(GC)]
        w0_loaded = sem("w0_loaded")
        w0b_loaded = sem("w0b_loaded")
        w0_ready = sem("w0_ready")
        w1_loaded = [sem(f"w1_loaded_{i}") for i in range(2)]
        w1h_ready = sem("w1h_ready")
        w1l_ready = sem("w1l_ready")
        w2_loaded = [sem(f"w2_loaded_{i}") for i in range(W2RING)]
        bias_sums_ready = sem("bias_sums_ready")
        xi_loaded = [sem(f"xi_loaded_{i}") for i in range(2)]
        xs_loaded = [sem(f"xs_loaded_{i}") for i in range(ZRING)]
        z_ready = sem("z_ready")
        z_used = sem("z_used")
        x1_ready = sem("x1_ready")
        x1_split = sem("x1_split")
        x1_summed = sem("x1_summed")
        x1_sums_ready = sem("x1_sums_ready")
        x0t_done = sem("x0t_done")
        x0t_ready = sem("x0t_ready")
        y_done = sem("y_done")
        y_act = sem("y_act")
        y_dve = sem("y_dve")
        x2_step = sem("x2_step")
        x0bd_ready = sem("x0bd_ready")
        s2_done = sem("s2_done")
        s2_ready = sem("s2_ready")
        g_done = sem("g_done")
        g_ready = sem("g_ready")
        w2_used = sem("w2_used")
        x3_ready = sem("x3_ready")
        top_loaded = sem("top_loaded")
        h_done = sem("h_done")
        h_ready = sem("h_ready")
        y_stored = sem("y_stored")

        block = ctx.enter_context(nc.Block())

        def run_chunks(eng, chunk):
            chunk(0, 0, 0)
            with eng.Fori(0, NG - 1) as g:
                for c in range(1, GC + 1):
                    chunk(g, c, None)
            for c in range(1, GC):
                chunk(NG - 1, c, GC * (NG - 1) + c)

        def scale_of(par, q, f):
            col = (q // 2) * FIELDS + f
            return x0t_sb[:, par, q % 2, col:col + 1]

        @block.sync
        def _(sp):
            sp.dma_start(ids_sb, ids).then_inc(ids_loaded, 16)
            sp.dma_start(w0_sb[:], w0a).then_inc(w0_loaded, 16)
            sp.dma_start(w0b_sb, w0b).then_inc(w0b_loaded, 16)
            for half in range(2):
                h = FIELDS // 2
                sp.dma_start(w1_raw[:, half * h:(half + 1) * h, :], w1[:, half * h:(half + 1) * h, :])\
                    .then_inc(w1_loaded[half], 16)
            sp.dma_start(b1_sb[:], b1_row.to_broadcast([P, H])).then_inc(b1_loaded, 16)

            def store_x0(uses, s):
                sp.wait_ge(gathered[s], 16 * GATHERS * uses)
                for b2 in range(2):
                    cols = slice(b2 * NC // 2, (b2 + 1) * NC // 2)
                    src = xg[b2 * FIELDS:(b2 + 1) * FIELDS, s, :].unsqueeze(1).to_broadcast([FIELDS, 2, NC // 2])
                    sp.dma_start(x0_dram[s, :, cols].rearrange("(copy f) n -> f copy n", f=FIELDS), src)\
                        .then_inc(x0_stored[s], 16)

            def load_xi(s, par):
                for s2 in range(2):
                    sp.dma_start(xi[s2 * FIELDS:(s2 + 1) * FIELDS, par, :],
                                 x0_dram[s, 0:FIELDS, :]).then_inc(xi_loaded[par], 16)

            def load_xs(s, r):
                tiles = item_tiles(r)
                for s2 in range(1 if r == 0 else 2):
                    first = s2 + 2 * tiles[0]
                    src = x0_dram[s, first:first + FIELDS, :]
                    src = bass.AP(src.tensor, src.offset, [[NC, FIELDS], [2 * NC, len(tiles)], [1, NC]])
                    sp.dma_start(xs[s2 * FIELDS:(s2 + 1) * FIELDS, r % ZRING, 0:len(tiles), :], src)\
                        .then_inc(xs_loaded[r % ZRING], 16 if r else 32)

            def load_chunk(g, c, items, first=False):
                s = c % GC
                if items[0] == 0:
                    sp.wait_ge(x0_stored[s], 32 * g + 32 * (c // GC + 1))
                    load_xi(s, c % 2)
                for r in items:
                    if not (first and r < ZRING):
                        sp.wait_ge(z_ready, at(g, c, ITEMS, r - ZRING + 1))
                    load_xs(s, r)

            store_x0(1, 0)
            load_chunk(0, 0, range(ITEMS), True)
            store_x0(1, 1)
            load_chunk(0, 1, range(ZRING))

            def chunk(g, c, k):
                if k != NCHUNK - 1:
                    load_chunk(g, c + 1, range(ZRING, ITEMS))
                if not (k is not None and k + 2 >= NCHUNK):
                    store_x0(g + (c + 2) // GC + 1, (c + 2) % GC)
                    load_chunk(g, c + 2, range(ZRING))

            run_chunks(sp, chunk)

            sp.wait_ge(z_ready, ITEMS * NCHUNK)
            sp.dma_start(wt1_sb, wt1[0:3 * H, :].rearrange("(k p) m -> p k m", p=H)).then_inc(top_loaded, 16)
            sp.dma_start(wt1d_sb, wt1[3 * H:3 * H + DENSE, :]).then_inc(top_loaded, 16)
            sp.dma_start(wt2_sb, wt2.rearrange("(k p) m -> p k m", p=P)).then_inc(top_loaded, 16)
            sp.dma_start(dense_sb, dense_t).then_inc(top_loaded, 16)
            sp.wait_ge(h_ready, M1 + M2 + 1)
            sp.dma_start(out.rearrange("b a -> a b"), y_sb).then_inc(y_stored, 16)
            sp.wait_ge(y_stored, 16)

        @block.gpsimd
        def _(pool):
            pool.wait_ge(rows_ready, 1)

            def gather(chunk, copies, s):
                nc.gpsimd.tensor_copy(rows_chunk[:, s, :], rows_sb[:, bass.ds(GATHERS * chunk, GATHERS)])\
                    .then_inc(rows_copied, 1)
                pool.wait_ge(rows_copied, copies)
                nc.gpsimd.tensor_tensor(carrier[:], vmax, voff, ALU.add)
                for j in range(GATHERS):
                    nc.gpsimd.indirect_dma_start(
                        out=xg[:, s, j * DIM:(j + 1) * DIM], out_offset=None, in_=table,
                        in_offset=bass.IndirectOffsetOnAxis(ap=rows_chunk[:, s, j:j + 1], axis=0))\
                        .then_inc(gathered[s], 16)

            for c in range(GC):
                gather(c, c + 1, c)

            with pool.Fori(0, NG - 1) as g:
                for c in range(GC):
                    pool.wait_ge(x0t_done, GC * g + c + 1)
                    pool.wait_ge(x0_stored[c], 32 * g + 32)
                    gather(GC * g + c + GC, GC * g + c + GC + 1, c)

        @block.scalar
        def _(act):
            act.dma_start(const_sb[:], consts).then_inc(const_loaded, 16)
            act.dma_start(params_sb[:], params).then_inc(params_loaded, 16)

            def load_w2(p):
                act.dma_start(w2_sb[:, p % W2RING, :, :], w2[:, p * W2F:(p + 1) * W2F, :])\
                    .then_inc(w2_loaded[p % W2RING], 16)

            act.wait_ge(params_loaded, 16)
            nc.scalar.mul(bias_sums[:], bias, float(DIM)).then_inc(bias_sums_ready, 1)
            for p in range(W1P):
                fs = slice(p * FIELDS // W1P, (p + 1) * FIELDS // W1P)
                act.wait_ge(w1_loaded[2 * p // W1P], 16)
                nc.scalar.activation(w1h[:, fs, :], w1_raw[:, fs, :], ACT.Copy).then_inc(w1h_ready, 1)

            def copy_x0t(par, done):
                act.wait_ge(x0t_done, done)
                nc.scalar.activation(x0t_sb[:, par, :, :].rearrange("p m c -> p (m c)"), x0t_ps, ACT.Copy)\
                    .then_inc(x0t_ready, 1)

            def make_x1(g, c):
                act.wait_ge(z_used, at(g, c, ITEMS, 2 * ITEMS))
                nc.scalar.activation(x1h[:, (c + 1) % 2, :], acc0[:], ACT.Identity, bias=bias[:, 0:1])\
                    .then_inc(x1_ready, 1)

            copy_x0t(0, 1)
            make_x1(0, -1)

            def copy_g(g, c, q):
                act.wait_ge(g_done, at(g, c, NQ, q + 1 - NQ))
                bank = g_last_ps[q % 2] if isinstance(g, int) and GC * g + c == NCHUNK else g_ps
                b = (c - 1) % GC * CB + q * GPQ
                nc.scalar.activation(g_sb[:, :, b:b + GPQ].rearrange("p f b -> p b f"),
                                     bank[:].rearrange("p (b f) -> p b f", f=FIELDS),
                                     ACT.Copy).then_inc(g_ready, 1)

            def copy_s2(g, c):
                act.wait_ge(s2_done, at(g, c, 1, 0))
                nc.scalar.activation(sums[:, 1, bass.ds(at(g, c, CB, -CB), CB)], s2_ps, ACT.Copy)\
                    .then_inc(s2_ready, 1)

            def copy_x3(g):
                act.wait_ge(w2_used, W2P * g + W2P)
                nc.scalar.activation(sums[:, 2, bass.ds(GB * g, GB)], x3_ps, ACT.Identity,
                                     bias=bias_sums[:, 2:3]).then_inc(x3_ready, 1)

            def chunk(g, c, k):
                par = c % 2
                act.wait_ge(x0t_ready, at(g, c, 1, 1))
                for j in range(BATCHES):
                    q, b = j // PERQ, j % PERQ
                    if q > 0:
                        act.wait_ge(x2_step, steps_before(g, c, q - 1, f"add{max(b, 1)}", done=True))
                    elif k != 0:
                        act.wait_ge(x2_step, steps_before(g, c - 1, NQ - 1, f"add{max(b, 1)}", done=True))
                    for i in range(3):
                        act.wait_ge(y_done, at(g, c, UNITS, 4 * j + i + 1))
                        for n in range(UF):
                            f = UF * (4 * b + i) + n
                            last = nc.scalar.activation(batch_sb[:, b, i, n * H:(n + 1) * H],
                                                        y_act_ps[i][:, n * H:(n + 1) * H], ACT.Copy,
                                                        scale=scale_of(par, q, f))
                        last.then_inc(y_act, 1)
                        for p in range(W2P - W2RING):
                            if c == GC and (W2_AFTER[p] + 1, W2_AFTER[p] + 2)[W2_AFTER[p] % 4 == 2] == 4 * j + i:
                                act.wait_ge(w2_used, W2P * g + p + 1)
                                load_w2(p + W2RING)
                    if k != 0 and j in COPY_G_AFTER:
                        if COPY_G_AFTER[j] == 0:
                            copy_s2(g, c)
                        copy_g(g, c, COPY_G_AFTER[j])
                    if k != NCHUNK - 1 and j == COPY_X0T_AFTER:
                        if k != 0:
                            act.wait_ge(x0bd_ready, at(g, c, NQ, 0))
                        copy_x0t(1 - par, at(g, c, 1, 2))
                    if k != NCHUNK - 1 and j == X1_AFTER:
                        make_x1(g, c)
                    if (c == GC or k == NCHUNK - 1) and j == 0:
                        for p in range(W2RING):
                            load_w2(p)
                    if c == GC and j == X3_AFTER:
                        copy_x3(g)

            run_chunks(act, chunk)

            act.wait_ge(x2_step, LAST_BLOCK)
            for i in range(1, W2P // W2RING):
                n = W2RING * W2F
                act.dma_start(w2_rest[:, (i - 1) * n:i * n, :], w2[:, i * n:(i + 1) * n, :])\
                    .then_inc(w2_rest_loaded[i - 1], 16)
            copy_s2(NG - 1, GC)
            for q in range(NQ):
                copy_g(NG - 1, GC, q)
            copy_x3(NG - 1)

            for m in range(M1):
                act.wait_ge(h_done, m + 1)
                nc.scalar.activation(h1_sb[:, m, :], h1_ps[m][:], ACT.Relu, bias=bt_sb[:, m:m + 1])\
                    .then_inc(h_ready, 1)
            for m in range(M2):
                act.wait_ge(h_done, M1 + m + 1)
                nc.scalar.activation(h2_sb[:, m, :], h2_ps[m][:], ACT.Relu, bias=bt_sb[:, M1 + m:M1 + m + 1])\
                    .then_inc(h_ready, 1)
            act.wait_ge(h_done, M1 + M2 + 1)
            nc.scalar.activation(y_sb, y_ps, ACT.Copy).then_inc(h_ready, 1)

        @block.vector
        def _(dve):
            dve.wait_ge(ids_loaded, 16)
            dve.wait_ge(const_loaded, 16)
            nc.vector.tensor_scalar(rows_sb[:], ids_sb, vmax, voff, ALU.min, ALU.add).then_inc(rows_ready, 1)
            dve.wait_ge(w0_loaded, 16)
            dve.wait_ge(w0b_loaded, 16)
            nc.vector.tensor_tensor(w0_sb[FIELDS:P, 0, :], w0_sb[FIELDS:P, 0, :], w0b_sb[FIELDS:P, 0, :], ALU.add)
            nc.vector.tensor_tensor(w0_sb[:, 1:T0 - 1, :], w0_sb[:, 1:T0 - 1, :], w0b_sb[:, 1:T0 - 1, :], ALU.add)\
                .then_inc(w0_ready, 1)
            for p in range(W1P):
                fs = slice(p * FIELDS // W1P, (p + 1) * FIELDS // W1P)
                dve.wait_ge(w1h_ready, p + 1)
                nc.vector.tensor_tensor(w1l[:, fs, :], w1_raw[:, fs, :], w1h[:, fs, :].bitcast(F32), ALU.subtract)\
                    .then_inc(w1l_ready, 1)

            def make_item(g, c, r, first):
                par = (c + 1) % 2
                if r == 0:
                    dve.wait_ge(xi_loaded[par], 32 * (GC // 2) * g + 32 * ((c + 1) // 2 + 1))
                per = ITEMS // ZRING
                dve.wait_ge(xs_loaded[r % ZRING], at(g, c, 32 * per, 32 * (per + r // ZRING + 1)))
                if not (first and r < ZRING):
                    dve.wait_ge(z_used, at(g, c, ITEMS, ITEMS + r - ZRING + 1))
                tiles = len(item_tiles(r))
                rows = FIELDS if r == 0 else P
                nc.vector.tensor_tensor(z[0:rows, r % ZRING, 0:tiles, :],
                                        xi[0:rows, par, :].unsqueeze(1).to_broadcast([rows, tiles, NC]),
                                        xs[0:rows, r % ZRING, 0:tiles, :], ALU.mult).then_inc(z_ready, 1)

            def split_x1(g, c):
                par = (c + 1) % 2
                dve.wait_ge(x1_ready, at(g, c, 1, 2))
                nc.vector.scalar_tensor_tensor(out=x1l[:, par, :], in0=acc0[:], scalar=bias[:, 0:1],
                                               in1=x1h[:, par, :].bitcast(F32), op0=ALU.add, op1=ALU.subtract)\
                    .then_inc(x1_split, 1)
                nc.vector.tensor_reduce(sums[:, 0, bass.ds(at(g, c, CB, CB), CB)],
                                        acc0[:].rearrange("p (b d) -> p b d", d=DIM),
                                        AX_X, ALU.add).then_inc(x1_summed, 1)

            for r in range(ITEMS):
                make_item(0, -1, r, True)
            split_x1(0, -1)
            for r in range(ZRING):
                make_item(0, 0, r, False)
            dve.wait_ge(b1_loaded, 16)

            def wait_step(g, c, q, name):
                place, needs = STEPS[name]
                first = isinstance(g, int) and GC * g + c == 0 and q == 0
                if not (first and name == "add1"):
                    dve.wait_ge(x2_step, steps_before(g, c, q, name) - (0 if first else place - needs))

            def fold0():
                nc.vector.tensor_reduce(part[:], acc[:].rearrange("p s (f o) -> p o (s f)", o=H), AX_X, ALU.add)\
                    .then_inc(x2_step, 1)

            def fold1(par, q):
                nc.vector.tensor_tensor(x2t[:, par, q, :], part[:], b1_sb[:], ALU.add).then_inc(x2_step, 1)

            def make_bd(g, c, q):
                par = (c - 1) % 2
                if q >= 2 or isinstance(g, int) and GC * g + c == NCHUNK:
                    dve.wait_ge(g_done, at(g, c, NQ, q - 1 - NQ))
                col = q // 2 * FIELDS
                nc.vector.tensor_tensor(
                    x0bd[:, q % 2, :, :],
                    x0t_sb[:, par, q % 2, col:col + FIELDS].unsqueeze(1).to_broadcast([P, GPQ, FIELDS]),
                    mask.unsqueeze(2).to_broadcast([P, GPQ, FIELDS]), ALU.mult).then_inc(x0bd_ready, 1)

            def chunk(g, c, k):
                par = c % 2
                dve.wait_ge(x0t_ready, at(g, c, 1, 1))
                for j in range(BATCHES):
                    q, b = j // PERQ, j % PERQ
                    dve.wait_ge(y_act, at(g, c, 3 * BATCHES, 3 * j + 1))
                    dve.wait_ge(y_done, at(g, c, UNITS, 4 * j + 4))
                    for n in range(UF):
                        f = UF * (4 * b + 3) + n
                        slot = batch_sb[:, b, 0, n * H:(n + 1) * H]
                        last = nc.vector.scalar_tensor_tensor(
                            out=slot, in0=y_dve_ps[j % 2][:, n * H:(n + 1) * H], scalar=scale_of(par, q, f),
                            in1=slot, op0=ALU.mult, op1=ALU.add)
                    last.then_inc(y_dve, 1)
                    folds = k != 0 or q > 0
                    if folds and b == 0:
                        wait_step(g, c, q, "fold0")
                        fold0()
                    elif folds and b == 1:
                        wait_step(g, c, q, "fold1")
                        fold1(par if q > 0 else 1 - par, (q - 1) % NQ)
                    if j in MAKE_ITEM_AFTER:
                        r = MAKE_ITEM_AFTER[j]
                        ahead = 1 if r < ZRING else 0
                        if not (k is not None and k + 1 + ahead >= NCHUNK):
                            make_item(g, c + ahead, r, False)
                    if b > 0:
                        dve.wait_ge(y_act, at(g, c, 3 * BATCHES, 3 * j + 3))
                        dve.wait_ge(y_dve, at(g, c, BATCHES, j + 1))
                        wait_step(g, c, q, f"add{b}")
                        nc.vector.tensor_tensor(acc[:], batch_sb[:, 0, :, :] if b == 1 else acc[:],
                                                batch_sb[:, b, :, :], ALU.add).then_inc(x2_step, 1)
                    if k != 0:
                        for e in MAKE_BD_AFTER.get(j, ()):
                            make_bd(g, c, e)
                    if k == NCHUNK - 1 and j >= BATCHES - 4 and j < BATCHES - 2:
                        make_bd(g, c + 1, j - (BATCHES - 4))
                    if k != NCHUNK - 1 and j == SPLIT_X1_AFTER:
                        split_x1(g, c)
                    if k == NCHUNK - 1 and j == SPLIT_X1_AFTER:
                        dve.wait_ge(x1_summed, NCHUNK)
                        dve.wait_ge(bias_sums_ready, 1)
                        nc.vector.tensor_scalar(sums[:, 0, :], sums[:, 0, :], bias_sums[:, 0:1], None, ALU.add)\
                            .then_inc(x1_sums_ready, 1)

            run_chunks(dve, chunk)
            dve.wait_ge(x2_step, LAST_BLOCK)
            fold0()
            dve.wait_ge(x2_step, LAST_BLOCK + 1)
            fold1((NCHUNK - 1) % 2, NQ - 1)
            for q in range(2, NQ):
                make_bd(NG - 1, GC, q)

        @block.tensor
        def _(pe):
            pe.wait_ge(w0_ready, 1)

            def use_item(g, c, r):
                pe.wait_ge(z_ready, at(g, c, ITEMS, ITEMS + r + 1))
                tiles = item_tiles(r)
                rows = FIELDS if r == 0 else P
                for n, t in enumerate(tiles):
                    mm = nc.tensor.matmul(acc0[:], w0_sb[0:rows, t, :], z[0:rows, r % ZRING, n, :],
                                          start=(r == 0), stop=(r == ITEMS - 1 and n == len(tiles) - 1))
                mm.then_inc(z_used, 1)

            def transpose_x0(s, uses):
                pe.wait_ge(gathered[s], 16 * GATHERS * uses)
                for m in range(2):
                    mm = nc.tensor.transpose(x0t_ps[:, m * P:(m + 1) * P], xg[:, s, m * P:(m + 1) * P], ident)
                mm.then_inc(x0t_done, 1)

            pe.wait_ge(const_loaded, 16)
            transpose_x0(0, 1)
            for r in range(ITEMS):
                use_item(0, -1, r)
            pe.wait_ge(w1l_ready, W1P)
            pe.wait_ge(w1h_ready, W1P)

            def make_g(g, c, q):
                par = (c - 1) % 2
                last = isinstance(g, int) and GC * g + c == NCHUNK
                bank = g_last_ps[q % 2] if last else g_ps
                if q == 0:
                    pe.wait_ge(x2_step, LAST_BLOCK + FOLDS if last else steps_before(g, c, 0, "fold1", done=True))
                    for e in range(NQ):
                        mm = nc.tensor.matmul(s2_ps[:, e * GPQ:(e + 1) * GPQ], x2t[:, par, e, :], mask,
                                              start=True, stop=True)
                    mm.then_inc(s2_done, 1)
                elif not (last and q == 1):
                    pe.wait_ge(g_ready, at(g, c, NQ, q - NQ - (1 if last else 0)))
                pe.wait_ge(x0bd_ready, at(g, c, NQ, q + 1 - NQ))
                nc.tensor.matmul(bank[:], x2t[:, par, q, :], x0bd[:, q % 2, :, :].rearrange("p b f -> p (b f)"),
                                 start=True, stop=True).then_inc(g_done, 1)

            def use_w2(g, p):
                if p == 0:
                    pe.wait_ge(g_ready, NQ * GC * g + NQ * GC)
                rest = isinstance(g, int) and p >= W2RING
                if not rest:
                    pe.wait_ge(w2_loaded[p % W2RING], 16 * (W2P // W2RING) * g + 16 * (p // W2RING + 1))
                elif p % W2RING == 0:
                    pe.wait_ge(w2_rest_loaded[p // W2RING - 1], 16)
                for n in range(W2F):
                    f = p * W2F + n
                    w = w2_rest[:, f - W2RING * W2F, :] if rest else w2_sb[:, p % W2RING, n, :]
                    mm = nc.tensor.matmul(x3_ps, w, g_sb[:, f, :],
                                          start=(f == 0), stop=(f == FIELDS - 1))
                mm.then_inc(w2_used, 1)

            def chunk(g, c, k):
                par = c % 2
                pe.wait_ge(x1_split, at(g, c, 1, 1))
                for u in range(UNITS):
                    q, j, bank = u // (4 * PERQ), u // 4, u % 4
                    fs = slice(UF * (u % (4 * PERQ)), UF * (u % (4 * PERQ)) + UF)
                    if bank < 3:
                        y_ps = y_act_ps[bank]
                        if not (k == 0 and j == 0):
                            pe.wait_ge(y_act, at(g, c, 3 * BATCHES, 3 * (j - 1) + bank + 1))
                    else:
                        y_ps = y_dve_ps[j % 2]
                        if not (k == 0 and j < 2):
                            pe.wait_ge(y_dve, at(g, c, BATCHES, j - 1))
                    cols = slice(q * P, (q + 1) * P)
                    nc.tensor.matmul(y_ps[:], x1h[:, par, cols], w1h[:, fs, :].rearrange("h f o -> h (f o)"),
                                     start=True, stop=False)
                    nc.tensor.matmul(y_ps[:], x1h[:, par, cols], w1l[:, fs, :].rearrange("h f o -> h (f o)"),
                                     start=False, stop=False)
                    nc.tensor.matmul(y_ps[:], x1l[:, par, cols], w1h[:, fs, :].rearrange("h f o -> h (f o)"),
                                     start=False, stop=True).then_inc(y_done, 1)
                    if k != NCHUNK - 1 and u in ITEM_AFTER:
                        if ITEM_AFTER[u] == 0:
                            pe.wait_ge(x1_summed, at(g, c, 1, 1))
                        use_item(g, c, ITEM_AFTER[u])
                    if k != 0 and u in G_AFTER:
                        make_g(g, c, G_AFTER[u])
                    if k != NCHUNK - 1 and u == X0T_AFTER:
                        transpose_x0((c + 1) % GC, g + (c + 1) // GC + 1)
                    if c == GC and u in W2_AFTER:
                        use_w2(g, W2_AFTER.index(u))

            run_chunks(pe, chunk)

            def top1(m, n):
                mm = nc.tensor.matmul(h1_ps[m][:], wt1_sb[:, n, m * P:(m + 1) * P], sums[:, n, :],
                                      start=False, stop=(n == 2))
                if n == 2:
                    mm.then_inc(h_done, 1)

            pe.wait_ge(top_loaded, 64)
            pe.wait_ge(x1_sums_ready, 1)
            for m in range(M1):
                if m < M1 - 1:
                    pe.wait_ge(y_act, 3 * BATCHES * NCHUNK - 2 + m)
                else:
                    pe.wait_ge(y_dve, BATCHES * NCHUNK - 1)
                nc.tensor.matmul(h1_ps[m][:], wt1d_sb[:, m * P:(m + 1) * P], dense_sb, start=True, stop=False)
                top1(m, 0)
            for q in range(NQ):
                make_g(NG - 1, GC, q)
                if q > 0:
                    pe.wait_ge(s2_ready, NCHUNK)
                    top1(q - 1, 1)
            top1(M1 - 1, 1)
            for p in range(W2P):
                use_w2(NG - 1, p)
            pe.wait_ge(x3_ready, NG)
            for m in range(M1):
                top1(m, 2)
            pe.wait_ge(y_dve, BATCHES * NCHUNK)
            for n in range(M1):
                pe.wait_ge(h_ready, n + 1)
                for m in range(M2):
                    mm = nc.tensor.matmul(h2_ps[m][:], wt2_sb[:, n, m * P:(m + 1) * P], h1_sb[:, n, :],
                                          start=(n == 0), stop=(n == M1 - 1))
                    if n == M1 - 1:
                        mm.then_inc(h_done, 1)
            for m in range(M2):
                pe.wait_ge(h_ready, M1 + m + 1)
                mm = nc.tensor.matmul(y_ps, wt3_sb[:, m:m + 1], h2_sb[:, m, :], start=(m == 0), stop=(m == M2 - 1))
            mm.then_inc(h_done, 1)


def kernel(**inputs):
    import numpy as _np
    import concourse.bacc as _bacc
    from concourse import mybir as _mybir
    from concourse.bass_utils import run_bass_kernel_spmd as _run

    tables = [_np.asarray(inputs[f"tbl_{f}"]) for f in range(FIELDS)]
    sizes = [t.shape[0] for t in tables]
    ids = _np.asarray(inputs["ids"]).reshape(NCHUNK, 2, GATHERS, FIELDS)
    w0 = _np.asarray(inputs["L0_rec_W0"]).reshape(H, FIELDS, FIELDS)
    w1 = _np.asarray(inputs["L0_rec_W1"]).reshape(H, H, FIELDS)
    w2 = _np.asarray(inputs["L0_rec_W2"]).reshape(H, H, FIELDS)

    first = _np.tile(_np.arange(FIELDS), 2 * T0)
    second = (first + _np.repeat(_np.arange(2 * T0), FIELDS)) % FIELDS
    w0a = w0[:, first, second].reshape(H, T0, P).transpose(2, 1, 0)
    w0b = w0[:, second, first].reshape(H, T0, P).transpose(2, 1, 0)[:, :T0 - 1]

    consts = _np.zeros((P, GPQ + P + 2), _np.float32)
    consts[_np.arange(P), _np.arange(P) // DIM] = 1.0
    consts[_np.arange(P), GPQ + _np.arange(P)] = 1.0
    starts = [sum(sizes[:f]) for f in range(FIELDS)]
    consts[:, GPQ + P] = _np.tile([n - 1 for n in sizes], 2)
    consts[:, GPQ + P + 1] = _np.tile(starts, 2)

    def column(a):
        return _np.asarray(a).reshape(-1, P).T

    laid = {
        "ids": ids.transpose(1, 3, 0, 2).reshape(P, NCHUNK * GATHERS),
        "table": _np.concatenate(tables, axis=0),
        "dense_t": _np.asarray(inputs["dense_ctx"]).T,
        "consts": consts,
        "params": _np.concatenate([column(inputs[n]) for n in (
            "L0_rec_b0", "L0_rec_b1", "L0_rec_b2", "b_top1", "b_top2", "W_top3")], axis=1),
        "b1_row": _np.asarray(inputs["L0_rec_b1"]).reshape(1, H),
        "w0a": w0a, "w0b": w0b,
        "w1": w1.transpose(1, 2, 0),
        "w2": w2.transpose(1, 2, 0), "wt1": inputs["W_top1"], "wt2": inputs["W_top2"],
    }
    nc = _bacc.Bacc("TRN2", target_bir_lowering=False, num_devices=1)
    arrays, args = {}, []
    for name, a in laid.items():
        a = _np.ascontiguousarray(a)
        arrays[f"in_{name}"] = a
        args.append(nc.dram_tensor(f"in_{name}", a.shape, _mybir.dt.from_np(a.dtype), kind="ExternalInput").ap())
    args.append(nc.dram_tensor("out_y", (BATCH, 1), _mybir.dt.float32, kind="ExternalOutput").ap())
    cin_tower(nc, *args)
    r = _run(nc, [arrays], core_ids=[0])
    return r.results[0]["out_y"]
```
